# Optimizing a Trainium2 kernel written in Bass

```python
import numpy as np
import jax
import jax.numpy as jnp

def _softmax(x, axis=-1):
    return jax.nn.softmax(x, axis=axis)

def _gelu(x):
    return jax.nn.gelu(x, approximate=True)

def _silu(x):
    return jax.nn.silu(x)

def _sigmoid(x):
    return jax.nn.sigmoid(x)

def _layernorm(x, axis=-1, eps=1e-05):
    m = jnp.mean(x, axis=axis, keepdims=True)
    v = jnp.var(x, axis=axis, keepdims=True)
    return (x - m) / jnp.sqrt(v + eps)

def _scatter_add(tgt, idx, src, axis=0):
    return tgt.at[idx].add(src)

def _segment_sum(src, seg, n):
    return jax.ops.segment_sum(src, seg, n)
kernel_name = 'mk_adj_ffn_d1_adj_r2_5c47db'

def setup_inputs(seed: int=0):
    np.random.seed(seed)
    _w = jnp.asarray

    def _rec_inputs():
        import jax
        import jax.numpy as jnp
        _gk = jax.random.key(seed)
        x = -0.0005207 + 1.001 * jax.random.normal(jax.random.fold_in(_gk, 1), (2048, 256), jnp.float32)
        _a = jax.random.bernoulli(jax.random.fold_in(_gk, 2), 0.00390625, (2048, 2048))
        adj = _a.astype(jnp.int32)
        _nm = jnp.ones((2048,), dtype=bool)
        nodemask = jnp.where(_nm, 1.0, 0.0).astype(jnp.int32)
        return (x, adj, nodemask)
    x, adj, nodemask = _rec_inputs()

    def _L0_gnn_setup():
        import jax, jax.numpy as jnp
        import numpy as np
        D = 256
        H = 8
        HD = D // H
        EPS = 1e-05
        NEG = -1e+30

        def layer_norm(x, scale, bias):
            mu = jnp.mean(x, axis=-1, keepdims=True)
            var = jnp.mean(jnp.square(x - mu), axis=-1, keepdims=True)
            return (x - mu) * jax.lax.rsqrt(var + EPS) * scale + bias
        key = jax.random.key(seed)
        ks = jax.random.split(key, 16)
        S = T = 2048
        inp = {'h_source': jax.random.normal(ks[0], (S, D), jnp.float32), 'h_target': jax.random.normal(ks[1], (T, D), jnp.float32), 'edge_mask': jax.random.randint(ks[2], (T, S), 0, 2, jnp.int32), 'source_mask': jnp.ones((S,), jnp.int32), 'target_mask': jnp.ones((T,), jnp.int32), 'ln1_scale': jnp.ones((D,), jnp.float32), 'ln1_bias': jnp.zeros((D,), jnp.float32), 'Wq': jax.random.normal(ks[3], (D, D), jnp.float32) / np.sqrt(D), 'bq': jnp.zeros((D,), jnp.float32), 'Wk': jax.random.normal(ks[4], (D, D), jnp.float32) / np.sqrt(D), 'bk': jnp.zeros((D,), jnp.float32), 'Wv': jax.random.normal(ks[5], (D, D), jnp.float32) / np.sqrt(D), 'bv': jnp.zeros((D,), jnp.float32), 'Wo': jax.random.normal(ks[6], (D, D), jnp.float32) / np.sqrt(D), 'bo': jnp.zeros((D,), jnp.float32), 'ln2_scale': jnp.ones((D,), jnp.float32), 'ln2_bias': jnp.zeros((D,), jnp.float32), 'W1': jax.random.normal(ks[7], (D, 4 * D), jnp.float32) / np.sqrt(D), 'W2': jax.random.normal(ks[8], (4 * D, D), jnp.float32) / np.sqrt(4 * D)}
        return inp
    _L0_gnn_all = _L0_gnn_setup()
    _L0_gnn_in = {k: v for k, v in _L0_gnn_all.items() if k in ('h_target', 'ln1_scale', 'ln1_bias', 'Wq', 'bq', 'Wk', 'bk', 'Wv', 'bv', 'Wo', 'bo', 'ln2_scale', 'ln2_bias', 'W1', 'W2')}
    del _L0_gnn_all

    def _L0_ffn_setup():
        import jax, jax.numpy as jnp
        import numpy as np
        B, S, D = (8, 1024, 256)
        E, K, H = (8, 2, 1024)
        key = jax.random.key(seed)
        ks = jax.random.split(key, 6)
        scale = 0.02
        return {'x': jax.random.normal(ks[0], (B, S, D), dtype=jnp.float32), 'gate_w': jax.random.normal(ks[1], (E, D), dtype=jnp.float32) * scale, 'w1': jax.random.normal(ks[2], (E, H, D), dtype=jnp.float32) * scale, 'b1': jax.random.normal(ks[3], (E, H), dtype=jnp.float32) * scale, 'w2': jax.random.normal(ks[4], (E, D, H), dtype=jnp.float32) * scale, 'b2': jax.random.normal(ks[5], (E, D), dtype=jnp.float32) * scale}
    _L0_ffn_all = _L0_ffn_setup()
    _L0_ffn_in = {k: v for k, v in _L0_ffn_all.items() if k in ('gate_w', 'w1', 'b1', 'w2', 'b2')}
    del _L0_ffn_all
    return {'x': x, 'adj': adj, 'nodemask': nodemask, 'L0_gnn_h_target': _L0_gnn_in['h_target'], 'L0_gnn_ln1_scale': _L0_gnn_in['ln1_scale'], 'L0_gnn_ln1_bias': _L0_gnn_in['ln1_bias'], 'L0_gnn_Wq': _L0_gnn_in['Wq'], 'L0_gnn_bq': _L0_gnn_in['bq'], 'L0_gnn_Wk': _L0_gnn_in['Wk'], 'L0_gnn_bk': _L0_gnn_in['bk'], 'L0_gnn_Wv': _L0_gnn_in['Wv'], 'L0_gnn_bv': _L0_gnn_in['bv'], 'L0_gnn_Wo': _L0_gnn_in['Wo'], 'L0_gnn_bo': _L0_gnn_in['bo'], 'L0_gnn_ln2_scale': _L0_gnn_in['ln2_scale'], 'L0_gnn_ln2_bias': _L0_gnn_in['ln2_bias'], 'L0_gnn_W1': _L0_gnn_in['W1'], 'L0_gnn_W2': _L0_gnn_in['W2'], 'L0_ffn_gate_w': _L0_ffn_in['gate_w'], 'L0_ffn_w1': _L0_ffn_in['w1'], 'L0_ffn_b1': _L0_ffn_in['b1'], 'L0_ffn_w2': _L0_ffn_in['w2'], 'L0_ffn_b2': _L0_ffn_in['b2']}

def reference(x, adj, nodemask, L0_gnn_h_target, L0_gnn_ln1_scale, L0_gnn_ln1_bias, L0_gnn_Wq, L0_gnn_bq, L0_gnn_Wk, L0_gnn_bk, L0_gnn_Wv, L0_gnn_bv, L0_gnn_Wo, L0_gnn_bo, L0_gnn_ln2_scale, L0_gnn_ln2_bias, L0_gnn_W1, L0_gnn_W2, L0_ffn_gate_w, L0_ffn_w1, L0_ffn_b1, L0_ffn_w2, L0_ffn_b2):
    import jax
    import jax.numpy as jnp

    def _L0_gnn_ref(h_source, h_target, edge_mask, source_mask, target_mask, ln1_scale, ln1_bias, Wq, bq, Wk, bk, Wv, bv, Wo, bo, ln2_scale, ln2_bias, W1, W2):
        import jax, jax.numpy as jnp
        import numpy as np
        D = 256
        H = 8
        HD = D // H
        EPS = 1e-05
        NEG = -1e+30

        def layer_norm(x, scale, bias):
            mu = jnp.mean(x, axis=-1, keepdims=True)
            var = jnp.mean(jnp.square(x - mu), axis=-1, keepdims=True)
            return (x - mu) * jax.lax.rsqrt(var + EPS) * scale + bias
        smask = (source_mask == 1)[:, None]
        tmask = (target_mask == 1)[:, None]
        hs = layer_norm(h_source, ln1_scale, ln1_bias)
        ht = layer_norm(h_target, ln1_scale, ln1_bias)
        hs = jnp.where(smask, hs, 0.0)
        ht = jnp.where(tmask, ht, 0.0)
        T, S = (ht.shape[0], hs.shape[0])
        q = (ht @ Wq + bq).reshape(T, H, HD) / jnp.sqrt(jnp.float32(HD))
        k = (hs @ Wk + bk).reshape(S, H, HD)
        v = (hs @ Wv + bv).reshape(S, H, HD)
        logits = jnp.einsum('thd,shd->hts', q, k)
        logits = jnp.where(edge_mask[None] != 0, logits, NEG)
        probs = jax.nn.softmax(logits, axis=-1)
        ctx = jnp.einsum('hts,shd->thd', probs, v).reshape(T, D)
        attn = ctx @ Wo + bo
        attn = jnp.where(tmask, attn, 0.0)
        ht = ht + attn
        ht = layer_norm(ht, ln2_scale, ln2_bias)
        ht = jnp.where(tmask, ht, 0.0)
        ff = jax.nn.gelu(ht @ W1) @ W2
        return ht + ff

    def _L0_ffn_ref(x, gate_w, w1, b1, w2, b2):
        import jax, jax.numpy as jnp
        import numpy as np
        B, S, D = (8, 1024, 256)
        E, K, H = (8, 2, 1024)
        batch, seq, dim = x.shape
        x_flat = x.reshape(-1, dim)
        T = x_flat.shape[0]
        gate_logits = x_flat @ gate_w.T
        topk_vals, topk_idx = jax.lax.top_k(gate_logits, K)
        topk_w = jax.nn.softmax(topk_vals, axis=-1)
        comb = jnp.zeros((T, E), dtype=x_flat.dtype)
        comb = comb.at[jnp.arange(T)[:, None], topk_idx].add(topk_w)
        out = jnp.zeros_like(x_flat)
        for e in range(E):
            h = jax.nn.gelu(x_flat @ w1[e].T + b1[e], approximate=False)
            y = h @ w2[e].T + b2[e]
            out = out + comb[:, e:e + 1] * y
        return out.reshape(batch, seq, dim)
    x = x + _L0_gnn_ref(_layernorm(x, axis=-1), L0_gnn_h_target, adj, nodemask, nodemask, L0_gnn_ln1_scale, L0_gnn_ln1_bias, L0_gnn_Wq, L0_gnn_bq, L0_gnn_Wk, L0_gnn_bk, L0_gnn_Wv, L0_gnn_bv, L0_gnn_Wo, L0_gnn_bo, L0_gnn_ln2_scale, L0_gnn_ln2_bias, L0_gnn_W1, L0_gnn_W2)
    x = x + _L0_ffn_ref(_layernorm(x, axis=-1)[None], L0_ffn_gate_w, L0_ffn_w1, L0_ffn_b1, L0_ffn_w2, L0_ffn_b2)[0]
    return x

_drawn_inputs = setup_inputs


def setup_inputs(seed=0):
    import zlib

    import numpy as np

    out = dict(_drawn_inputs(seed))
    spreads = {'L0_gnn_ln1_scale': (1.0, 0.2),
     'L0_gnn_ln1_bias': (0.0, 0.1),
     'L0_gnn_bq': (0.0, 0.389),
     'L0_gnn_bk': (0.0, 2.0),
     'L0_gnn_bv': (0.0, 0.1),
     'L0_gnn_bo': (0.0, 0.1),
     'L0_gnn_ln2_scale': (1.0, 0.2),
     'L0_gnn_ln2_bias': (0.0, 0.1)}
    factors = {'L0_ffn_b1': 22.506, 'L0_ffn_b2': 7.93}
    for name, (base, spread) in spreads.items():
        noise = np.random.default_rng([zlib.crc32(name.encode()), seed]).standard_normal(out[name].shape)
        drawn = base * np.exp(spread * noise) if base else spread * noise
        out[name] = jnp.asarray(drawn.astype(out[name].dtype))
    for name, factor in factors.items():
        out[name] = (out[name] * factor).astype(out[name].dtype)
    return out
```

```python
from contextlib import ExitStack

import concourse.bass as bass
from concourse import mybir

ALU = mybir.AluOpType
ACT = mybir.ActivationFunctionType
AX = mybir.AxisListType
F32 = mybir.dt.float32
F32R = mybir.dt.float32r
BF16 = mybir.dt.bfloat16
F16 = mybir.dt.float16
I32 = mybir.dt.int32
U32 = mybir.dt.uint32

P = 128
EPS = 1e-5
NO_EDGE = -(2.0**100)
WSCALE = 64.0


def at_least(eng, sem, value):
    if not isinstance(value, int) or value > 0:
        eng.wait_ge(sem, value)


def graph_attention_and_experts(nc, x, adj, adjT, nodemask, h_target, ln1_scale, ln1_bias, Wq, bq, Wk, bk, Wv, bv,
                                Wo, bo, ln2_scale, ln2_bias, W1, W2, gate_wT, w1T, b1, w2T, b2, out):
    T, D = x.shape
    NT = T // P
    DC = D // P
    H = 8
    HD = D // H
    TB = 512
    NB = T // TB
    TPB = TB // P
    GT = 4
    NG = NT // GT
    QSCALE = float(HD) ** -0.5
    KR = 3 * HD
    F = W1.shape[1]
    FC = F // P
    E, _, HE = w1T.shape
    HC = HE // P

    ctx = ExitStack()
    with ctx:
        def sem(name):
            return ctx.enter_context(nc.semaphore(name))

        def sb(name, shape, dt, scope=ctx):
            return scope.enter_context(nc.sbuf_tensor(name, shape, dt))

        def dram(name, shape, dt):
            return nc.dram_tensor(name, shape, dt).ap()

        k_stack = dram("k_stack", [H, 3, HD, T], F32)
        q_stack = dram("q_stack", [H, 3, HD, T], F32)
        ht_rows = dram("ht_rows", [T, D], F32)
        ctx_cols = dram("ctx_cols", [D, T], F32)
        sums = dram("sums", [H, T], F32)
        inv_sums = dram("inv_sums", [H, T], F32)

        ps = ctx.enter_context(nc.psum_tensor("ps", [P, 8, 512], F32))
        ident = sb("ident", [P, P], F32)
        identb = sb("identb", [P, P], BF16)
        m01 = sb("m01", [P, NT], F32)
        minus_half = sb("minus_half", [P, NT], F32)

        const_ready = sem("const_ready")

        def wait_apart(eng, signal, value):
            if not isinstance(value, int):
                value = eng.to_reg(value)
            eng.wait_ge(const_ready, 3)
            eng.wait_ge(signal, value)

        ph1 = ExitStack()
        ph12 = ExitStack()
        ctx.enter_context(ph12)
        v_all = sb("v_all", [P, NT, H, 2, HD], F32, ph12)

        x_in = sem("x_in")
        h_in = sem("h_in")
        small_in = sem("small_in")
        w_in = sem("w_in")
        stat_step = sem("stat_step")
        var_ready = sem("var_ready")
        rstd_ready = sem("rstd_ready")
        dve_step = sem("dve_step")
        xn_scaled = sem("xn_scaled")
        hn_ready = sem("hn_ready")
        hn_scaled = sem("hn_scaled")
        hs_ready = sem("hs_ready")
        ht_ready = sem("ht_ready")
        tr_ready = sem("tr_ready")
        tr_copied = sem("tr_copied")
        kq_ready = sem("kq_ready")
        kq_high = sem("kq_high")
        kq_split = sem("kq_split")
        v_ready = sem("v_ready")
        v_ones = sem("v_ones")
        v_stored = sem("v_stored")
        kq_out = [sem("kq_out0"), sem("kq_out1")]
        ht_out = sem("ht_out")
        wq_scaled = sem("wq_scaled")
        pool_step = sem("pool_step")

        with ph1:
            def s1(name, shape, dt):
                return sb(name, shape, dt, ph1)
            xs = s1("xs", [P, NT, D], F32)
            hh = s1("hh", [P, NT, D], F32)
            sT = s1("sT", [P, 2, DC, GT * P], F32)
            kq_hi = s1("kq_hi", [P, 2, 512], F32R)
            kq_lo = s1("kq_lo", [P, 2, 512], F32R)
            wqkv = s1("wqkv", [P, 3, DC, D], F32)
            ln_s = s1("ln_s", [P, D], F32)
            ln_b = s1("ln_b", [P, D], F32)
            bv_b = s1("bv_b", [P, D], F32)
            bkq = s1("bkq", [P, 2, DC], F32)
            nm_i = s1("nm_i", [P, NT], I32)
            stats = s1("stats", [P, 3, NT, 6], F32)
            mean = s1("mean", [P, 3, NT], F32)
            var = s1("var", [P, 3, NT], F32)
            rstd = s1("rstd", [P, 3, NT], F32)
            tmp = s1("tmp", [P, 4, NT], F32)

            block = nc.Block()
            with block:
                @block.sync
                def _(sp):
                    sp.dma_start(xs[:, :, :], x.rearrange("(i p) d -> p i d", p=P)).then_inc(x_in, 16)
                    sp.dma_start(hh[:, :, :], h_target.rearrange("(i p) d -> p i d", p=P)).then_inc(h_in, 16)
                    sp.dma_start(ln_s[:, :], ln1_scale.partition_broadcast(P)).then_inc(small_in, 16)
                    sp.dma_start(ln_b[:, :], ln1_bias.partition_broadcast(P)).then_inc(small_in, 16)
                    sp.dma_start(nm_i[:, :], nodemask.rearrange("(i p) -> p i", p=P),
                                 allow_slow_non_contiguous=True).then_inc(small_in, 16)
                    sp.dma_start(bv_b[:, :], bv.partition_broadcast(P)).then_inc(small_in, 16)
                    for n, w in enumerate((Wk, Wq, Wv)):
                        sp.dma_start(wqkv[:, n, :, :], w.rearrange("(c p) n -> p c n", p=P)).then_inc(w_in, 16)
                    for n, w in enumerate((bk, bq)):
                        sp.dma_start(bkq[:, n, :], w.rearrange("(c p) -> p c", p=P),
                                     allow_slow_non_contiguous=True).then_inc(w_in, 16)
                    for n, stack in enumerate((k_stack, q_stack)):
                        with sp.Fori(0, NG) as g:
                            for c in range(DC):
                                sp.wait_ge(kq_split, n * NG * DC + DC * g + c + 1)
                                for r, part in enumerate((kq_hi, kq_lo, kq_hi) if n == 0 else (kq_hi, kq_hi, kq_lo)):
                                    sp.dma_start(stack[4 * c:4 * c + 4, r, :, bass.ds(g * 512, 512)],
                                                 part[:, c, :].bitcast(F32))\
                                        .then_inc(kq_out[c], 16)
                    sp.wait_ge(ht_ready, NT)
                    sp.dma_start(ht_rows.rearrange("(i p) d -> p i d", p=P), hh[:, :, :]).then_inc(ht_out, 16)
                    sp.wait_ge(ht_out, 16)
                    for c in range(DC):
                        sp.wait_ge(kq_out[c], 2 * NG * 3 * 16)

                @block.gpsimd
                def _(pool):
                    pool.memset(minus_half[:, :], -0.5).then_inc(const_ready, 1)
                    pool.memset(v_all[:, :, :, 1, :], 1.0).then_inc(v_ones, 1)
                    pool.memset(ident[:, :], 0.0).then_inc(pool_step, 1)
                    pool.memset(identb[:, :], 0.0).then_inc(pool_step, 1)
                    pool.wait_ge(pool_step, 2)
                    for m in (ident, identb):
                        pool.affine_select(out=m[:, :], in_=m[:, :], compare_op=ALU.not_equal, fill=1.0, base=0,
                                           pattern=[[-1, P]], channel_multiplier=1).then_inc(const_ready, 1)
                    pool.wait_ge(const_ready, 1)
                    for n in range(3):
                        pool.wait_ge(var_ready, n + 1)
                        pool.tensor_tensor(rstd[:, n, :], var[:, n, :], minus_half[:, :], ALU.pow)\
                            .then_inc(rstd_ready, 1)
                    pool.wait_ge(small_in, 64)
                    with pool.Fori(0, NT) as i:
                        pool.wait_ge(hn_ready, i + 1)
                        pool.tensor_tensor(hh[:, i, :], hh[:, i, :], ln_s[:, :], ALU.mult).then_inc(hn_scaled, 1)

                @block.vector
                def _(dve):
                    steps = [0]

                    def then(ins):
                        steps[0] += 1
                        ins.then_inc(stat_step, 1)
                        dve.wait_ge(stat_step, steps[0])

                    def moments(n):
                        e, o = stats[:, n, :, 1], stats[:, n, :, 4]
                        dve.tensor_tensor(tmp[:, 0, :], e, o, ALU.add)
                        dve.tensor_tensor(tmp[:, 1, :], e, o, ALU.subtract)
                        then(dve.tensor_tensor(tmp[:, 2, :], stats[:, n, :, 2], stats[:, n, :, 5], ALU.add))
                        dve.tensor_scalar(mean[:, n, :], tmp[:, 0, :], 0.5, None, ALU.mult)
                        then(dve.tensor_tensor(tmp[:, 3, :], tmp[:, 1, :], tmp[:, 1, :], ALU.mult))
                        then(dve.tensor_scalar(tmp[:, 3, :], tmp[:, 3, :], 0.25, EPS, ALU.mult, ALU.add))
                        dve.scalar_tensor_tensor(out=var[:, n, :], in0=tmp[:, 2, :], scalar=1.0 / D, in1=tmp[:, 3, :],
                                                 op0=ALU.mult, op1=ALU.add).then_inc(var_ready, 1)

                    for n, (src, arrived) in enumerate(((xs, x_in), (hh, h_in))):
                        dve.wait_ge(arrived, 16)
                        with dve.Fori(0, NT) as i:
                            dve.bn_stats(stats[:, n, i, :], src[:, i, :]).then_inc(dve_step, 1)
                        dve.wait_ge(dve_step, NT * (n + 1))
                        moments(n)
                        if n == 0:
                            dve.wait_ge(small_in, 64)
                            then(dve.tensor_scalar(m01[:, :], nm_i[:, :], 1.0, None, ALU.is_equal))
                            dve.wait_ge(w_in, 16 * 5)
                            dve.tensor_scalar(wqkv[:, 1, :, :], wqkv[:, 1, :, :], QSCALE, None, ALU.mult)\
                                .then_inc(wq_scaled, 1)
                            dve.tensor_scalar(bkq[:, 1, :], bkq[:, 1, :], QSCALE, None, ALU.mult)\
                                .then_inc(wq_scaled, 1)
                    dve.wait_ge(rstd_ready, 1)
                    with dve.Fori(0, NT) as i:
                        dve.tensor_scalar(xs[:, i, :], xs[:, i, :], mean[:, 0, bass.ds(i, 1)], rstd[:, 0, bass.ds(i, 1)],
                                          ALU.subtract, ALU.mult).then_inc(dve_step, 1)
                        dve.wait_ge(dve_step, 2 * NT + 2 * i + 1)
                        dve.bn_stats(stats[:, 2, i, :], xs[:, i, :]).then_inc(dve_step, 1)
                    dve.wait_ge(dve_step, 4 * NT)
                    moments(2)
                    dve.wait_ge(rstd_ready, 2)
                    then(dve.tensor_tensor(rstd[:, 1, :], rstd[:, 1, :], m01[:, :], ALU.mult))
                    with dve.Fori(0, NT) as i:
                        dve.tensor_scalar(hh[:, i, :], hh[:, i, :], mean[:, 1, bass.ds(i, 1)], rstd[:, 1, bass.ds(i, 1)],
                                          ALU.subtract, ALU.mult).then_inc(hn_ready, 1)
                    dve.wait_ge(rstd_ready, 3)
                    then(dve.tensor_tensor(rstd[:, 2, :], rstd[:, 2, :], m01[:, :], ALU.mult))
                    base = 4 * NT
                    with dve.Fori(0, NT) as i:
                        dve.tensor_scalar(xs[:, i, :], xs[:, i, :], mean[:, 2, bass.ds(i, 1)], rstd[:, 2, bass.ds(i, 1)],
                                          ALU.subtract, ALU.mult).then_inc(dve_step, 1)
                        dve.wait_ge(dve_step, base + 2 * i + 1)
                        dve.tensor_tensor(xs[:, i, :], xs[:, i, :], ln_s[:, :], ALU.mult).then_inc(dve_step, 1)
                        dve.wait_ge(dve_step, base + 2 * i + 2)
                        dve.scalar_tensor_tensor(out=xs[:, i, :], in0=ln_b[:, :], scalar=m01[:, bass.ds(i, 1)],
                                                 in1=xs[:, i, :], op0=ALU.mult, op1=ALU.add).then_inc(hs_ready, 1)

                    def split_low(n, g):
                        for c in range(DC):
                            k = n * NG * DC + DC * g + c
                            dve.wait_ge(kq_high, k + 1)
                            dve.scalar_tensor_tensor(out=kq_lo[:, c, :], in0=ps[:, 2 + c, :], scalar=bkq[:, n, c:c + 1],
                                                     in1=kq_hi[:, c, :].bitcast(F32), op0=ALU.add, op1=ALU.subtract)\
                                .then_inc(kq_split, 1)

                    with dve.Fori(0, NG) as g:
                        split_low(0, g)
                        for i in range(GT):
                            dve.wait_ge(v_ready, GT * g + i + 1)
                            dve.tensor_tensor(v_all[:, GT * g + i, :, 0, :],
                                              ps[:, 4 + i, 0:D].rearrange("p (h d) -> p h d", d=HD),
                                              bv_b[:, :].rearrange("p (h d) -> p h d", d=HD), ALU.add)\
                                .then_inc(v_stored, 1)
                    with dve.Fori(0, NT) as i:
                        dve.wait_ge(hn_scaled, i + 1)
                        dve.scalar_tensor_tensor(out=hh[:, i, :], in0=ln_b[:, :], scalar=m01[:, bass.ds(i, 1)],
                                                 in1=hh[:, i, :], op0=ALU.mult, op1=ALU.add).then_inc(ht_ready, 1)
                    with dve.Fori(0, NG) as g:
                        split_low(1, g)

                @block.scalar
                def _(act):
                    act.wait_ge(w_in, 16 * 5)

                    for n in range(2):
                        if n:
                            act.wait_ge(wq_scaled, 2)
                        for g in range(NG):
                            k = n * NG + g
                            act.wait_ge(tr_ready, k + 1)
                            act.activation(sT[:, n, :, :], ps[:, 0:2, :], ACT.Copy).then_inc(tr_copied, 1)
                            for c in range(DC):
                                act.wait_ge(kq_ready, DC * k + c + 1)
                                at_least(act, kq_out[c], 48 * k)
                                act.activation(kq_hi[:, c, :], ps[:, 2 + c, :], ACT.Identity, bias=bkq[:, n, c:c + 1])\
                                    .then_inc(kq_high, 1)

                @block.tensor
                def _(pe):
                    pe.wait_ge(const_ready, 3)
                    pe.wait_ge(w_in, 16 * 5)

                    def turn(src, ready, n, g, first):
                        k = n * NG + g
                        for i in range(GT):
                            pe.wait_ge(ready, GT * g + i + 1)
                            if i == 0 and not first:
                                pe.wait_ge(tr_copied, k)
                            for c in range(DC):
                                mm = pe.transpose(ps[:, c, i * P:(i + 1) * P],
                                                  src[:, GT * g + i, c * P:(c + 1) * P], ident[:, :])
                        mm.then_inc(tr_ready, 1)
                        pe.wait_ge(tr_copied, k + 1)

                    def project(n, g, first):
                        k = n * NG + g
                        for c in range(DC):
                            if not first:
                                pe.wait_ge(kq_split, DC * (k - 1) + c + 1)
                            for j in range(DC):
                                mm = pe.matmul(ps[:, 2 + c, :], wqkv[:, n, j, c * P:(c + 1) * P], sT[:, n, j, :],
                                               start=(j == 0), stop=(j == DC - 1))
                            mm.then_inc(kq_ready, 1)

                    def values(g, first):
                        for i in range(GT):
                            if not first:
                                pe.wait_ge(v_stored, GT * (g - 1) + i + 1)
                            for j in range(DC):
                                mm = pe.matmul(ps[:, 4 + i, 0:D], sT[:, 0, j, i * P:(i + 1) * P], wqkv[:, 2, j, :],
                                               start=(j == 0), stop=(j == DC - 1))
                            mm.then_inc(v_ready, 1)

                    turn(xs, hs_ready, 0, 0, True)
                    project(0, 0, True)
                    values(0, True)
                    for g in range(1, NG):
                        turn(xs, hs_ready, 0, g, False)
                        project(0, g, False)
                        values(g, False)
                    pe.wait_ge(wq_scaled, 2)
                    for g in range(NG):
                        turn(hh, ht_ready, 1, g, False)
                        project(1, g, False)

        UNITS = TPB * T // 512
        UPT = T // 512
        maxima_scores = sem("maxima_scores")
        maxima_read = sem("maxima_read")
        negmax_ready = sem("negmax_ready")
        negmax_turned = sem("negmax_turned")
        shift_high = sem("shift_high")
        shift_split = sem("shift_split")
        shift_rows = [sem(f"shift_rows{i}") for i in range(4)]
        q_in = [sem(f"q_in{i}") for i in range(4)]
        k_in = [sem(f"k_in{i}") for i in range(H)]
        scores_ready = sem("scores_ready")
        weights_ready = sem("weights_ready")
        context_added = sem("context_added")
        part_ready = sem("part_ready")
        context_summed = sem("context_summed")
        context_out = [sem(f"context_out{i}") for i in range(2)]
        maskA_ready = sem("maskA_ready")
        maskB_ready = sem("maskB_ready")
        adjA_in = [sem(f"adjA_in{i}") for i in range(2)]
        adjB_in = [sem(f"adjB_in{i}") for i in range(2)]
        ones_ready = sem("ones_ready")

        ph2 = ExitStack()
        with ph2:
            def s2(name, shape, dt):
                return sb(name, shape, dt, ph2)
            ks = s2("ks", [KR + 2, H, T], F32R)
            qs = s2("qs", [KR + 2, 4, TB], F32R)
            maskA = s2("maskA", [P, TPB, T], BF16)
            maskB = s2("maskB", [P, 2, NT, TB], BF16)
            adjA = s2("adjA", [P, 2, T], I32)
            adjB = s2("adjB", [P, 2, 2, TB], I32)
            weights = s2("weights", [P, 2, 2, TB], F32)
            masked = s2("masked", [P, UPT, 512], BF16)
            piecemax = s2("piecemax", [P, 2, TPB, UPT], F32)
            negmax = s2("negmax", [P, 2, TPB], F32)
            shift_hi = s2("shift_hi", [TPB, 2, P], F32R)
            shift_lo = s2("shift_lo", [TPB, 2, P], F32R)
            credit = s2("credit", [P, 6], F32)
            part = s2("part", [2 * HD, TB], F32)
            total = s2("total", [2 * HD, 2, TB], F32)

            adj_t = adj.rearrange("(i p) s -> i p s", p=P)
            adjT_t = adjT.rearrange("(i p) t -> p i t", p=P)
            q_rows = q_stack.rearrange("h r d t -> h (r d) t")
            k_rows = k_stack.rearrange("h r d t -> h (r d) t")
            ctx_out = ctx_cols.rearrange("(h d) t -> h d t", d=HD)

            block = nc.Block()
            with block:
                @block.sync
                def _(sp):
                    def load_q(n, b, h):
                        sp.dma_start(qs[0:KR, h % 4, :].bitcast(F32), q_rows[h, :, bass.ds(b * TB, TB)])\
                            .then_inc(q_in[h % 4], 16)

                    def load_adjA(tile, a):
                        sp.dma_start(adjA[:, a % 2, :], adj_t[tile, :, :]).then_inc(adjA_in[a % 2], 16)

                    def load_adjB(b, h):
                        sp.dma_start(adjB[:, h % 2, :, :], adjT_t[:, 2 * h:2 * h + 2, bass.ds(b * TB, TB)])\
                            .then_inc(adjB_in[h % 2], 16)

                    def store_shift(n, h):
                        sp.wait_ge(shift_split, n + 1)
                        for r, rows in enumerate((shift_hi, shift_lo)):
                            sp.dma_start(qs[KR + r:KR + r + 1, h % 4, :].bitcast(F32), rows[:, h % 2, :].bitcast(F32))\
                                .then_inc(shift_rows[h % 4], 16)

                    def store_context(n, b, h):
                        wait_apart(sp, context_summed, n + 2)
                        at = bass.ds(b * TB, TB)
                        sp.dma_start(ctx_out[h, :, at], total[0:HD, h % 2, :]).then_inc(context_out[h % 2], 16)
                        sp.dma_start(sums[h:h + 1, at], total[HD:HD + 1, h % 2, :]).then_inc(context_out[h % 2], 16)

                    load_q(0, 0, 0)
                    sp.dma_start(ks[0:KR, 0, :].bitcast(F32), k_rows[0, :, :]).then_inc(k_in[0], 16)
                    for a in range(2):
                        load_adjA(a, a)
                    for h in range(1, 3):
                        load_q(h, 0, h)
                        sp.dma_start(ks[0:KR, h, :].bitcast(F32), k_rows[h, :, :]).then_inc(k_in[h], 16)
                    for a in range(2, TPB):
                        sp.wait_ge(maskA_ready, a - 1)
                        load_adjA(a, a)
                    for h in range(2):
                        load_adjB(0, h)
                    store_shift(0, 0)
                    for h in range(2, H):
                        sp.wait_ge(maskB_ready, h - 1)
                        load_adjB(0, h)
                    for h in range(3, H):
                        sp.dma_start(ks[0:KR, h, :].bitcast(F32), k_rows[h, :, :]).then_inc(k_in[h], 16)
                    with sp.Fori(0, NB) as b:
                        nxt = (b + 1) % NB
                        for h in range(H):
                            n = b * H + h
                            sp.wait_ge(scores_ready, n * 8 + 1)
                            load_q(n + 3, b if h + 3 < H else nxt, (h + 3) % H)
                            sp.wait_ge(maskB_ready, H + n - 1)
                            load_adjB(nxt, h)
                            if h in (H - 4, H - 3):
                                for a in range(2 * (h - H + 4), 2 * (h - H + 5)):
                                    sp.wait_ge(maskA_ready, TPB * (b + 1) + a - 1)
                                    load_adjA(nxt * TPB + a, a)
                            if h:
                                store_context(n - 1, b, h - 1)
                            store_shift(n + 1, (h + 1) % H)
                            if h == H - 1:
                                store_context(n, b, h)
                    for i in range(2):
                        sp.wait_ge(context_out[i], 16 + 32 * NB * H // 2)
                    for i in range(4):
                        sp.wait_ge(q_in[i], 16 * (NB * H // 4 + (1 if i < 3 else 0)))
                        sp.wait_ge(shift_rows[i], 32 * (NB * H // 4 + (1 if i == 0 else 0)))
                    for i in range(2):
                        sp.wait_ge(adjA_in[i], 16 * (NB + 1) * TPB // 2)
                        sp.wait_ge(adjB_in[i], 16 * (NB + 1) * H // 2)

                @block.vector
                def _(dve):
                    dve.memset(ks[KR:KR + 2, :, :].bitcast(F32), 1.0).then_inc(ones_ready, 1)
                    dve.memset(credit[:, 0:1], 0.0).then_inc(context_summed, 1)
                    for i in range(2):
                        dve.memset(credit[:, 1 + i:2 + i], 0.0).then_inc(context_added, 1)
                        dve.memset(credit[:, 3 + i:4 + i], 0.0).then_inc(context_out[i], 16)

                    def mask_a(b, a):
                        dve.wait_ge(adjA_in[a % 2], 16 * (b * (TPB // 2) + a // 2 + 1))
                        dve.tensor_scalar(maskA[:, a, :], adjA[:, a % 2, :], 0.0, NO_EDGE, ALU.is_equal, ALU.mult)\
                            .then_inc(maskA_ready, 1)

                    def mask_b(b, h):
                        dve.wait_ge(adjB_in[h % 2], 16 * (b * (H // 2) + h // 2 + 1))
                        dve.tensor_scalar(maskB[:, b % 2, 2 * h:2 * h + 2, :], adjB[:, h % 2, :, :], 0.0, NO_EDGE,
                                          ALU.is_equal, ALU.mult).then_inc(maskB_ready, 1)

                    def turned_shift(n, par):
                        dve.wait_ge(negmax_turned, n + 1)
                        turned = ps[0:TPB, 6 + par, 0:P]
                        dve.tensor_copy(shift_hi[:, par, :], turned).then_inc(shift_high, 1)
                        dve.wait_ge(shift_high, n + 1)
                        dve.tensor_tensor(shift_lo[:, par, :], turned, shift_hi[:, par, :].bitcast(F32),
                                          ALU.subtract).then_inc(shift_split, 1)

                    def add_halves(n, b, h):
                        dve.wait_ge(context_out[h % 2], 16 + 32 * (b * (H // 2) + h // 2))
                        dve.wait_ge(part_ready, n + 1)
                        dve.tensor_tensor(total[:, h % 2, :], ps[0:2 * HD, 6 + h % 2, :], part[:, :], ALU.add)\
                            .then_inc(context_summed, 1)

                    def maxima(n, par, beside):
                        for u in range(UNITS):
                            a, k = u // UPT, u % UPT
                            wait_apart(dve, maxima_scores, UNITS * n + u + 1)
                            dve.tensor_tensor_reduce(masked[:, k, :], ps[:, u % 2, :],
                                                     maskA[:, a, k * 512:(k + 1) * 512],
                                                     1.0, NO_EDGE, ALU.add, ALU.max,
                                                     piecemax[:, par, a, k:k + 1]).then_inc(maxima_read, 1)
                            if k == UPT - 1:
                                dve.wait_ge(maxima_read, UNITS * n + u + 1)
                                dve.tensor_reduce(negmax[:, par, a:a + 1], piecemax[:, par, a, :], AX.X, ALU.max,
                                                  negate=True).then_inc(negmax_ready, 1)
                            beside(u)

                    def step(n, b, h):
                        def beside(u):
                            if u == 1 and h:
                                add_halves(n - 1, b, h - 1)
                            elif u == 5:
                                dve.wait_ge(scores_ready, 8 * H * b + 1)
                                mask_b(b + 1, h)
                            elif u == 9:
                                turned_shift(n + 1, (h + 1) % 2)
                            if h == H - 3 and u % UPT == UPT - 1:
                                mask_a(b + 1, u // UPT)
                        if h == H - 2:
                            dve.wait_ge(maskA_ready, TPB * (b + 2))
                        maxima(n + 2, h % 2, beside)
                        if h == H - 1:
                            add_halves(n, b, h)

                    for a in range(TPB):
                        mask_a(0, a)
                    dve.wait_ge(maskA_ready, TPB)
                    maxima(0, 0, lambda u: None)
                    turned_shift(0, 0)
                    maxima(1, 1, lambda u: None)
                    for h in range(H):
                        mask_b(0, h)
                    with dve.Fori(0, NB) as b:
                        for h in range(H):
                            step(b * H + h, b, h)

                @block.scalar
                def _(act):
                    def copy_half(n, h):
                        act.wait_ge(context_added, 8 * n + 10)
                        act.wait_ge(context_summed, n + 1)
                        act.activation(part[:, :], ps[2 * HD:4 * HD, 6 + h % 2, :], ACT.Copy).then_inc(part_ready, 1)

                    act.wait_ge(ones_ready, 1)
                    act.activation(credit[0:2, 5:6], ks[KR:KR + 2, 0, 0:1].bitcast(F32), ACT.Copy)\
                        .then_inc(weights_ready, 1)
                    with act.Fori(0, NB) as b:
                        for h in range(H):
                            n = b * H + h
                            for j in range(8):
                                act.wait_ge(scores_ready, 8 * n + j + 1)
                                act.wait_ge(context_added, 8 * n + j + 1)
                                act.activation(weights[:, j % 2, :, :], ps[:, 2 + 2 * (j % 2):4 + 2 * (j % 2), :],
                                               ACT.Exp).then_inc(weights_ready, 1)
                                if j == 0 and h:
                                    copy_half(n - 1, h - 1)
                            if h == H - 1:
                                copy_half(n, h)

                @block.tensor
                def _(pe):
                    def piece(n, b, h, u):
                        a, k = u // UPT, u % UPT
                        if u == 0:
                            pe.wait_ge(q_in[h % 4], 16 * (b * (H // 4) + h // 4 + 1))
                            pe.wait_ge(k_in[h], 16)
                        at_least(pe, maxima_read, UNITS * n + u - 1)
                        pe.matmul(ps[:, u % 2, :], qs[0:KR, h % 4, a * P:(a + 1) * P],
                                  ks[0:KR, h, k * 512:(k + 1) * 512], start=True, stop=True)\
                            .then_inc(maxima_scores, 1)

                    def turn_negmax(n, h):
                        pe.wait_ge(negmax_ready, TPB * (n + 1))
                        pe.wait_ge(context_summed, n)
                        pe.transpose(ps[0:TPB, 6 + h % 2, 0:P], negmax[:, h % 2, :], ident[:, :])\
                            .then_inc(negmax_turned, 1)

                    def key_scores(n, b, h, j):
                        if j == 0:
                            pe.wait_ge(shift_rows[h % 4], 32 * (b * (H // 4) + h // 4 + 1))
                        if h == 0:
                            pe.wait_ge(maskB_ready, H * b + j + 1)
                        at_least(pe, weights_ready, 8 * n + j)
                        for i in range(2):
                            bank = ps[:, 2 + 2 * (j % 2) + i, :]
                            pe.matmul(bank, ks[:, h, (2 * j + i) * P:(2 * j + i + 1) * P], qs[:, h % 4, :],
                                      start=True, stop=False)
                            mm = pe.matmul(bank, identb[:, :], maskB[:, b % 2, 2 * j + i, :], start=False, stop=True)
                        mm.then_inc(scores_ready, 1)

                    def add_context(n, h, j):
                        pe.wait_ge(weights_ready, 8 * n + j + 2)
                        for i in range(2):
                            mm = pe.matmul(ps[2 * i * HD:2 * (i + 1) * HD, 6 + h % 2, :],
                                           v_all[:, 2 * j + i, h, :, :].rearrange("p t d -> p (t d)"),
                                           weights[:, j % 2, i, :],
                                           start=(j == 0), stop=(j == 7), tile_position=(0, 2 * i * HD))
                        mm.then_inc(context_added, 1)

                    pe.wait_ge(ones_ready, 1)
                    pe.wait_ge(v_ones, 1)
                    for u in range(UNITS):
                        piece(0, 0, 0, u)
                    pe.wait_ge(negmax_ready, TPB)
                    pe.transpose(ps[0:TPB, 6, 0:P], negmax[:, 0, :], ident[:, :]).then_inc(negmax_turned, 1)
                    for u in range(UNITS):
                        piece(1, 0, 1, u)
                    key_scores(0, 0, 0, 0)
                    with pe.Fori(0, NB) as b:
                        for h in range(H):
                            n = b * H + h
                            b1_, h1 = (b, h + 1) if h + 1 < H else (b + 1, 0)
                            b2_, h2 = (b, h + 2) if h + 2 < H else (b + 1, h + 2 - H)
                            for j in range(8):
                                piece(n + 2, b2_, h2, 2 * j)
                                if j < 7:
                                    key_scores(n, b, h, j + 1)
                                else:
                                    key_scores(n + 1, b1_, h1, 0)
                                piece(n + 2, b2_, h2, 2 * j + 1)
                                add_context(n, h, j)
                                if j == 3:
                                    turn_negmax(n + 1, h1)
        ph12.close()

        TOPK = 2
        NBLK = TOPK * T // P + E
        REGION = T + P
        ROW = 272
        expert_rows = dram("expert_rows", [E * REGION + P, ROW], F32)
        sum_rows = dram("sum_rows", [T + P, D], F32)
        assert (F, HE) == (1024, 1024)
        SETS = E + 1
        SPLIT3 = 6
        WC = DC * HE

        ph34 = ExitStack()
        ctx.enter_context(ph34)

        def s34(name, shape, dt):
            return sb(name, shape, dt, ph34)
        wall = s34("wall", [P, SETS, 2, 2, WC], F16)
        wst = s34("wst", [P, 2, WC], F32)
        pad = s34("pad", [P, ROW], F32)
        b1s = s34("b1s", [P, E, HC], F32)
        b2b = s34("b2b", [P, E, D], F32)
        table = s34("table", [P, 2, NBLK + 2], I32)
        c_in = sem("c_in")
        wst_in = [sem("wst_in0"), sem("wst_in1")]
        wst_high = [sem("wst_high0"), sem("wst_high1")]
        wst_split = [sem("wst_split0"), sem("wst_split1")]

        def up(s, part, c, m):
            return wall[:, s, 0, part, c * HE + m * P:c * HE + (m + 1) * P]

        def down(s, part, m):
            return wall[:, s, 1, part, m * D:(m + 1) * D]

        def load_stage(sp, s, n):
            sp.wait_ge(wst_split[n], s)
            sp.dma_start(wst[:, n, :].rearrange("p (c n) -> p c n", n=(HE, D)[n]),
                         (w1T, w2T)[n][s - 1, :, :].rearrange("(c p) n -> p c n", p=P)).then_inc(wst_in[n], 16)

        def stage_high(act, s, n):
            act.wait_ge(wst_in[n], 16 * s + 16)
            act.activation(wall[:, s, n, 0, :], wst[:, n, :], ACT.Copy, scale=WSCALE).then_inc(wst_high[n], 1)

        def stage_low(dve, s, n):
            dve.wait_ge(wst_high[n], s + 1)
            dve.scalar_tensor_tensor(out=wall[:, s, n, 1, :], in0=wst[:, n, :], scalar=WSCALE,
                                     in1=wall[:, s, n, 0, :], op0=ALU.mult, op1=ALU.subtract)\
                .then_inc(wst_split[n], 1)

        def beside(p, i, bb):
            return 1 + 3 * bb + (3 * p + i) // 2, (3 * p + i) % 2

        ph3 = ExitStack()
        with ph3:
            def s3(name, shape, dt):
                return sb(name, shape, dt, ph3)
            spare = wall[:, SETS - 2:SETS, :, :, :].rearrange("p s n h c -> p (s n h c)").bitcast(F32)
            at = [0]

            def from_spare(*shape):
                size = 1
                for d in shape:
                    size *= d
                v = spare[:, at[0]:at[0] + size]
                at[0] += size
                return v.rearrange("p (a b) -> p a b", a=shape[0]) if len(shape) == 2 else \
                    v.rearrange("p (a b c) -> p a b c", a=shape[0], b=shape[1])
            cT = from_spare(DC, TB)
            rT = from_spare(DC, TB)
            htb = from_spare(2, TPB, D)
            xb = from_spare(2, TPB, D)
            g32 = from_spare(2, TB)
            xnT = from_spare(DC, TB)
            assert at[0] <= spare.shape[1]
            inv = s3("inv", [P, H * T // P], F32)
            wo = s3("wo", [P, DC, D], F32)
            gw = s3("gw", [P, DC, E], F32)
            bo_b = s3("bo_b", [P, D], F32)
            s2_b = s3("s2_b", [P, D], F32)
            sh2_b = s3("sh2_b", [P, D], F32)
            hT = s3("hT", [P, 2, 2, DC, TB], F16)
            gT = s3("gT", [P, 2, 2, TB], F16)
            rows = s3("rows", [P, TPB, ROW], F32)
            st3 = s3("st3", [P, 2, TPB, 6], F32)
            mo3 = s3("mo3", [P, 2, 8, TPB], F32)
            logits = s3("logits", [P, TPB, E], F32)
            top = s3("top", [P, 2, TPB], F32)
            key = s3("key", [P, TPB, E], F32)
            keymax = s3("keymax", [P, TPB], F32)
            gap = s3("gap", [P, 5, TPB], F32)
            hot = s3("hot", [P, 2, TPB, E], F32)
            wgt = s3("wgt", [P, 2, TPB, E], F32)
            member = s3("member", [P, TPB, E], BF16)
            rank = s3("rank", [P, TPB, E], F32)
            picked = s3("picked", [P, 2, TPB, E], F32)
            slotf = s3("slotf", [P, 2, TPB], F32)
            slots = s3("slots", [P, 2, TPB], U32)
            place = s3("place", [P, E], F32)
            down_from_e = s3("down_from_e", [P, E], F32)
            u3 = s3("u3", [P, TPB, D], F32)
            y3 = s3("y3", [P, TPB, D], F32)
            credit3 = s3("credit3", [P, 8], F32)
            region0 = s3("region0", [P, E], F32)
            tokens = s3("tokens", [P, NT], F32)
            blocks = s3("blocks", [P, NBLK + 2], F32)
            before = s3("before", [P, P], BF16)
            onesb = s3("onesb", [P, P], BF16)
            minus_half4 = minus_half[:, 0:TPB]
            nblk = s3("nblk", [P, 4, E], F32)
            counts = s3("counts", [P, 3, E], I32)
            ends = s3("ends", [P, E], F32)
            past = s3("past", [P, 2, NBLK + 2, E], F32)
            tabf = s3("tabf", [P, 5, NBLK + 2], F32)

            wsmall_in = sem("wsmall_in")
            ctx_in = sem("ctx_in")
            sums_in = sem("sums_in")
            inv_ready = sem("inv_ready")
            inv_out = sem("inv_out")
            inv_in = sem("inv_in")
            ctx_scaled = sem("ctx_scaled")
            h3_in = [sem("h3_in0"), sem("h3_in1")]
            x3_in = [sem("x3_in0"), sem("x3_in1")]
            c3_step = sem("c3_step")
            c3_ready = sem("c3_ready")
            attn_ready = sem("attn_ready")
            link_a = sem("link_a")
            link_t = sem("link_t")
            link_e = sem("link_e")
            var3 = [sem("var3A"), sem("var3T")]
            rstd3 = [sem("rstd3A"), sem("rstd3T")]
            h2_ready = sem("h2_ready")
            h2_scaled = sem("h2_scaled")
            h2T_ready = sem("h2T_ready")
            h2T_high = sem("h2T_high")
            h2T_split = sem("h2T_split")
            up_ready = sem("up_ready")
            gelu_ready = sem("gelu_ready")
            g_high = sem("g_high")
            g_split = sem("g_split")
            down_done = sem("down_done")
            x1_ready = sem("x1_ready")
            x1_out = [sem("x1_out0"), sem("x1_out1")]
            xn_ready = sem("xn_ready")
            xnT_ready = sem("xnT_ready")
            xnT_copied = sem("xnT_copied")
            gates_ready = sem("gates_ready")
            gates_read = sem("gates_read")
            rank_read = sem("rank_read")
            gap_ready = sem("gap_ready")
            gap_exp = sem("gap_exp")
            member_ready = sem("member_ready")
            rows_ready = sem("rows_ready")
            rank_ready = sem("rank_ready")
            slots_ready = sem("slots_ready")
            scattered = sem("scattered")
            table_ready = sem("table_ready")
            pads_out = sem("pads_out")

            block = nc.Block()
            with block:
                @block.sync
                def _(sp):
                    def load_inv(b):
                        for h in range(H):
                            at = h % (H // DC) * HD
                            sp.dma_start(rT[at:at + HD, h // (H // DC), :],
                                         inv_sums[h, bass.ds(b * TB, TB)].partition_broadcast(HD)).then_inc(inv_in, 16)

                    compact = "h (c t) -> (h c) t"
                    sp.dma_start(inv[:, :], sums.rearrange(compact, t=H * T // P)).then_inc(sums_in, 16)
                    sp.dma_start(cT[:, :, :], ctx_cols[:, 0:TB].rearrange("(c p) t -> p c t", p=P)).then_inc(ctx_in, 16)
                    sp.dma_start(wo[:, :, :], Wo.rearrange("(c p) n -> p c n", p=P)).then_inc(wsmall_in, 16)
                    sp.dma_start(bo_b[:, :], bo.partition_broadcast(P)).then_inc(wsmall_in, 16)

                    def load_h(b, p):
                        sp.dma_start(htb[:, p, :, :], ht_rows[bass.ds(b * TB, TB), :]
                                     .rearrange("(a p) d -> p a d", p=P)).then_inc(h3_in[p], 16)

                    def load_x(b, p):
                        sp.dma_start(xb[:, p, :, :], x[bass.ds(b * TB, TB), :]
                                     .rearrange("(a p) d -> p a d", p=P)).then_inc(x3_in[p], 16)
                    load_h(0, 0)
                    sp.dma_start(s2_b[:, :], ln2_scale.partition_broadcast(P)).then_inc(wsmall_in, 16)
                    sp.dma_start(sh2_b[:, :], ln2_bias.partition_broadcast(P)).then_inc(wsmall_in, 16)
                    sp.dma_start(gw[:, :, :], gate_wT.rearrange("(c p) e -> p c e", p=P)).then_inc(wsmall_in, 16)
                    sp.wait_ge(inv_ready, 1)
                    sp.dma_start(inv_sums.rearrange(compact, t=H * T // P), inv[:, :]).then_inc(inv_out, 16)
                    sp.wait_ge(inv_out, 16)
                    load_inv(0)
                    for n, w in enumerate((W1, W2)):
                        sp.dma_start(wst[:, n, :].rearrange("p (c n) -> p c n", n=(F, D)[n]),
                                     w.rearrange("(c p) n -> p c n", p=P)).then_inc(wst_in[n], 16)
                    load_x(0, 0)
                    load_h(1, 1)
                    load_x(1, 1)
                    sp.dma_start(b1s[:, :, :], b1).then_inc(c_in, 16)
                    sp.dma_start(b2b[:, :, :], b2.rearrange("e d -> (e d)").partition_broadcast(P)).then_inc(c_in, 16)
                    def load_context(b, at):
                        wait_apart(sp, attn_ready, TPB * b)
                        sp.dma_start(cT[:, :, :], ctx_cols[:, bass.ds(at * TB, TB)]
                                     .rearrange("(c p) t -> p c t", p=P)).then_inc(ctx_in, 16)
                        load_inv(at)

                    def store_x1(b, bb, p):
                        sp.wait_ge(x1_ready, TPB * (b + 1) + 1)
                        load_h((b + 2) % NB, p)
                        sp.dma_start(sum_rows[bass.ds(b * TB, TB), :].rearrange("(a p) d -> p a d", p=P),
                                     xb[:, p, :, :]).then_inc(x1_out[p], 16)
                        sp.wait_ge(x1_out[p], 16 * (bb + 1))
                        sp.wait_ge(xn_ready, TPB * (b + 1))
                        load_x((b + 2) % NB, p)

                    load_context(1, 1)
                    with sp.Fori(0, NB // 2) as bb:
                        for p in range(2):
                            b = 2 * bb + p
                            load_context(b + 2, (b + 2) % NB)
                            for i in range(3):
                                if p and i == 2:
                                    store_x1(b - 1, bb, 0)
                                load_stage(sp, *beside(p, i, bb))
                            if p:
                                store_x1(b, bb, 1)
                    sp.wait_ge(table_ready, 1)
                    for e in range(E):
                        r = sp.value_load(counts[0:1, 0, e:e + 1], min_val=0, max_val=T)
                        sp.dma_start(expert_rows[bass.ds(r + e * REGION, P), :], pad[:, :]).then_inc(pads_out, 16)
                    sp.wait_ge(pads_out, 16 * E)
                    sp.wait_ge(ctx_in, 16 * (NB + 2))
                    sp.wait_ge(inv_in, 16 * H * (NB + 2))
                    sp.wait_ge(c_in, 32)
                    for p in range(2):
                        sp.wait_ge(h3_in[p], 16 * (NB // 2 + 1))
                        sp.wait_ge(x3_in[p], 16 * (NB // 2 + 1))

                @block.gpsimd
                def _(pool):
                    pool.memset(pad[:, :], 0.0).then_inc(c3_step, 1)
                    pool.wait_ge(c3_step, 1)
                    pool.iota(pad[:, D + E:D + E + 1], pattern=[[0, 1]], base=T, channel_multiplier=1,
                              allow_small_or_imprecise_dtypes=True).then_inc(c3_ready, 1)
                    pool.iota(tokens[:, :], pattern=[[P, NT]], base=0, channel_multiplier=1,
                              allow_small_or_imprecise_dtypes=True).then_inc(c3_ready, 1)
                    pool.iota(down_from_e[:, :], pattern=[[-1, E]], base=E, channel_multiplier=0,
                              allow_small_or_imprecise_dtypes=True).then_inc(c3_ready, 1)
                    pool.iota(region0[:, :], pattern=[[REGION, E]], base=0, channel_multiplier=0,
                              allow_small_or_imprecise_dtypes=True).then_inc(c3_ready, 1)
                    pool.iota(blocks[:, :], pattern=[[1, NBLK + 2]], base=0, channel_multiplier=0,
                              allow_small_or_imprecise_dtypes=True).then_inc(c3_ready, 1)
                    pool.memset(onesb[:, :], 1.0).then_inc(c3_ready, 1)
                    pool.memset(rows[:, :, D + E:ROW], 0.0).then_inc(c3_ready, 1)
                    pool.wait_ge(c3_ready, 7)
                    pool.affine_select(out=before[:, :], in_=onesb[:, :], compare_op=ALU.is_gt, fill=0.0, base=0,
                                       pattern=[[1, P]], channel_multiplier=-1).then_inc(c3_ready, 1)

                    pool.wait_ge(c3_ready, 8)
                    pool.dma_start(expert_rows[E * REGION:E * REGION + P, :], pad[:, :]).then_inc(scattered, 16)

                    def inverse_root(k, b):
                        pool.wait_ge(var3[k], b + 1)
                        pool.tensor_tensor(mo3[:, k, 7, :], mo3[:, k, 6, :], minus_half[:, 0:TPB], ALU.pow)\
                            .then_inc(rstd3[k], 1)

                    def scatter(b):
                        wait_apart(pool, rows_ready, 2 * b + 2)
                        pool.wait_ge(slots_ready, 2 * b + 2)
                        for a in range(TPB):
                            for k in range(TOPK):
                                pool.indirect_dma_start(
                                    out=expert_rows[:, :], in_=rows[:, a, :], in_offset=None,
                                    out_offset=bass.IndirectOffsetOnAxis(ap=slots[:, k, a:a + 1], axis=0),
                                    bounds_check=E * REGION + P - 1).then_inc(scattered, 16)

                    def scale_context(b):
                        pool.wait_ge(ctx_in, 16 * b + 16)
                        pool.wait_ge(inv_in, 16 * H * (b + 1))
                        pool.tensor_tensor(cT[:, :, :], cT[:, :, :], rT[:, :, :], ALU.mult).then_inc(ctx_scaled, 1)

                    scale_context(0)
                    inverse_root(0, 0)
                    scale_context(1)
                    with pool.Fori(0, NB // 2) as bb:
                        b = 2 * bb
                        inverse_root(0, b + 1)
                        scale_context(b + 2)
                        inverse_root(1, b)
                        inverse_root(0, b + 2)
                        scale_context(b + 3)
                        scatter(b)
                        inverse_root(1, b + 1)
                        scatter(b + 1)
                    pool.wait_ge(scattered, 16 * (TOPK * NT + 1))

                @block.vector
                def _(dve):
                    def chain(signal, length):
                        at_block, marked = [0], [0]

                        def begin(b):
                            at_block[0], marked[0] = b, 0

                        def mark(ins):
                            marked[0] += 1
                            ins.then_inc(signal, 1)

                        def settle():
                            dve.wait_ge(signal, length * at_block[0] + marked[0])

                        def end():
                            assert marked[0] == length, (marked[0], length)
                        return begin, mark, settle, end

                    A_LEN = 4 * TPB + 7
                    T_LEN = 2 * TPB + 26
                    begin_A, mark_A, settle_A, end_A = chain(link_a, A_LEN)
                    begin_T, mark_T, settle_T, end_T = chain(link_t, T_LEN)

                    def moments(k, mark, settle):
                        m = mo3[:, k, :, :]
                        e, o = st3[:, k, :, 1], st3[:, k, :, 4]
                        mark(dve.tensor_tensor(m[:, 0, :], e, o, ALU.add))
                        mark(dve.tensor_tensor(m[:, 1, :], e, o, ALU.subtract))
                        mark(dve.tensor_tensor(m[:, 2, :], st3[:, k, :, 2], st3[:, k, :, 5], ALU.add))
                        settle()
                        mark(dve.tensor_scalar(m[:, 3, :], m[:, 0, :], 0.5, None, ALU.mult))
                        mark(dve.tensor_tensor(m[:, 4, :], m[:, 1, :], m[:, 1, :], ALU.mult))
                        settle()
                        mark(dve.tensor_scalar(m[:, 5, :], m[:, 4, :], 0.25, EPS, ALU.mult, ALU.add))
                        settle()
                        dve.scalar_tensor_tensor(out=m[:, 6, :], in0=m[:, 2, :], scalar=1.0 / D, in1=m[:, 5, :],
                                                 op0=ALU.mult, op1=ALU.add).then_inc(var3[k], 1)

                    def attention_sum(b, p, at, loads):
                        begin_A(b)
                        dve.wait_ge(h3_in[p], loads)
                        for a in range(TPB):
                            dve.wait_ge(attn_ready, TPB * b + 2 * (a // 2) + 2)
                            mark_A(dve.tensor_tensor(u3[:, a, :], ps[:, 2 + a // 2, a % 2 * D:(a % 2 + 1) * D],
                                                          bo_b[:, :], ALU.add))
                        settle_A()
                        for a in range(TPB):
                            mark_A(dve.scalar_tensor_tensor(out=htb[:, p, a, :], in0=u3[:, a, :],
                                                                 scalar=m01[:, bass.ds(at + a, 1)],
                                                                 in1=htb[:, p, a, :], op0=ALU.mult, op1=ALU.add))
                        settle_A()
                        for a in range(TPB):
                            mark_A(dve.bn_stats(st3[:, 0, a, :], htb[:, p, a, :]))
                        settle_A()
                        moments(0, mark_A, settle_A)

                    def second_norm(b, p, at):
                        dve.wait_ge(rstd3[0], b + 1)
                        mark_A(dve.tensor_tensor(mo3[:, 0, 5, :], mo3[:, 0, 7, :], m01[:, bass.ds(at, TPB)],
                                                      ALU.mult))
                        settle_A()
                        for a in range(TPB):
                            mark_A(dve.tensor_scalar(u3[:, a, :], htb[:, p, a, :], mo3[:, 0, 3, a:a + 1],
                                                          mo3[:, 0, 5, a:a + 1], ALU.subtract, ALU.mult))
                        settle_A()
                        for a in range(TPB):
                            dve.tensor_tensor(u3[:, a, :], u3[:, a, :], s2_b[:, :], ALU.mult).then_inc(h2_scaled, 1)
                        dve.wait_ge(h2_scaled, TPB * b + TPB)
                        for a in range(TPB):
                            dve.scalar_tensor_tensor(out=htb[:, p, a, :], in0=sh2_b[:, :],
                                                     scalar=m01[:, bass.ds(at + a, 1)], in1=u3[:, a, :],
                                                     op0=ALU.mult, op1=ALU.add).then_inc(h2_ready, 1)
                        end_A()

                    def split_turned(b, p):
                        for c in range(DC):
                            dve.wait_ge(h2T_high, DC * b + c + 1)
                            dve.tensor_tensor(hT[:, p, 1, c, :], ps[:, 2 + c, :], hT[:, p, 0, c, :], ALU.subtract)\
                                .then_inc(h2T_split, 1)

                    def split_hidden(b, f):
                        dve.wait_ge(g_high, FC * b + f + 1)
                        dve.tensor_tensor(gT[:, 1, f % 2, :], g32[:, f % 2, :], gT[:, 0, f % 2, :], ALU.subtract)\
                            .then_inc(g_split, 1)

                    def new_x(b, bb, p):
                        begin_T(b)
                        dve.wait_ge(down_done, FC * b + FC + 2)
                        for a in range(TPB):
                            mark_T(dve.scalar_tensor_tensor(out=y3[:, a, :], in0=ps[:, 4 + a, 0:D],
                                                                 scalar=1.0 / WSCALE, in1=htb[:, p, a, :],
                                                                 op0=ALU.mult, op1=ALU.add))
                        settle_T()
                        dve.wait_ge(x3_in[p], 16 * (bb + 1))
                        for a in range(TPB):
                            dve.tensor_tensor(xb[:, p, a, :], xb[:, p, a, :], y3[:, a, :], ALU.add)\
                                .then_inc(x1_ready, 1)
                        dve.wait_ge(x1_ready, TPB * b + TPB + 1)

                    def new_moments(p):
                        for a in range(TPB):
                            mark_T(dve.bn_stats(st3[:, 1, a, :], xb[:, p, a, :]))
                        settle_T()
                        moments(1, mark_T, settle_T)

                    def expert_rows_of(b, p):
                        dve.wait_ge(rstd3[1], b + 1)
                        dve.wait_ge(scattered, 16 * TOPK * TPB * b + 16)
                        for a in range(TPB):
                            dve.tensor_scalar(rows[:, a, 0:D], xb[:, p, a, :], mo3[:, 1, 3, a:a + 1],
                                              mo3[:, 1, 7, a:a + 1], ALU.subtract, ALU.mult).then_inc(xn_ready, 1)

                    def choose(b):
                        mark = mark_T
                        dve.wait_ge(gates_ready, b + 1)
                        dve.tensor_copy(logits[:, :, :], ps[:, 2, 0:TPB * E].rearrange("p (a e) -> p a e", e=E))\
                            .then_inc(gates_read, 1)
                        dve.wait_ge(gates_read, b + 2)
                        for k in range(TOPK):
                            mark(dve.tensor_reduce(top[:, k, :], logits[:, :, :], AX.X, ALU.max))
                            settle_T()
                            mark(dve.tensor_tensor(key[:, :, :], logits[:, :, :],
                                                   top[:, k, :].unsqueeze(2).to_broadcast([P, TPB, E]), ALU.is_equal))
                            settle_T()
                            mark(dve.tensor_tensor(key[:, :, :], key[:, :, :],
                                                   down_from_e[:, :].unsqueeze(1).to_broadcast([P, TPB, E]),
                                                   ALU.mult))
                            settle_T()
                            mark(dve.tensor_reduce(keymax[:, :], key[:, :, :], AX.X, ALU.max))
                            settle_T()
                            mark(dve.tensor_tensor(hot[:, k, :, :], key[:, :, :],
                                                   keymax[:, :].unsqueeze(2).to_broadcast([P, TPB, E]), ALU.is_equal))
                            settle_T()
                            if k == 0:
                                mark(dve.scalar_tensor_tensor(out=logits[:, :, :], in0=hot[:, 0, :, :], scalar=-3e38,
                                                              in1=logits[:, :, :], op0=ALU.mult, op1=ALU.add))
                                settle_T()
                        dve.tensor_tensor(member[:, :, :], hot[:, 0, :, :], hot[:, 1, :, :], ALU.add)\
                            .then_inc(member_ready, 1)
                        dve.tensor_tensor(gap[:, 0, :], top[:, 1, :], top[:, 0, :], ALU.subtract)\
                            .then_inc(gap_ready, 1)

                    def send(b):
                        mark = mark_T
                        dve.wait_ge(gap_exp, b + 1)
                        mark(dve.tensor_scalar(gap[:, 2, :], gap[:, 1, :], 1.0, None, ALU.add))
                        settle_T()
                        mark(dve.reciprocal(gap[:, 3, :], gap[:, 2, :]))
                        settle_T()
                        mark(dve.tensor_tensor(gap[:, 4, :], gap[:, 3, :], gap[:, 1, :], ALU.mult))
                        settle_T()
                        for k in range(TOPK):
                            mark(dve.tensor_tensor(wgt[:, k, :, :], hot[:, k, :, :],
                                                   gap[:, 3 + k, :].unsqueeze(2).to_broadcast([P, TPB, E]), ALU.mult))
                        settle_T()
                        dve.tensor_tensor(rows[:, :, D:D + E], wgt[:, 0, :, :], wgt[:, 1, :, :], ALU.add)\
                            .then_inc(rows_ready, 1)
                        dve.tensor_copy(rows[:, :, D + E], tokens[:, bass.ds(b * TPB, TPB)]).then_inc(rows_ready, 1)
                        dve.wait_ge(rank_ready, b + 1)
                        mark(dve.tensor_tensor(rank[:, :, :], ps[:, 3, 0:TPB * E].rearrange("p (a e) -> p a e", e=E),
                                               place[:, :].unsqueeze(1).to_broadcast([P, TPB, E]), ALU.add))
                        settle_T()
                        dve.tensor_tensor(place[:, :], place[:, :], ps[:, 3, TPB * E:(TPB + 1) * E], ALU.add)\
                            .then_inc(rank_read, 1)
                        for k in range(TOPK):
                            mark(dve.tensor_tensor(picked[:, k, :, :], hot[:, k, :, :], rank[:, :, :], ALU.mult))
                        settle_T()
                        mark(dve.tensor_reduce(slotf[:, :, :], picked[:, :, :, :], AX.X, ALU.add))
                        settle_T()
                        for k in range(TOPK):
                            dve.tensor_copy(slots[:, k, :], slotf[:, k, :]).then_inc(slots_ready, 1)
                        dve.wait_ge(rank_read, b + 2)
                        end_T()

                    dve.wait_ge(sums_in, 16)
                    dve.reciprocal(inv[:, :], inv[:, :]).then_inc(inv_ready, 1)
                    dve.wait_ge(c3_ready, 8)
                    dve.tensor_copy(place[:, :], region0[:, :]).then_inc(rank_read, 1)
                    dve.memset(credit3[:, 0:1], 0.0).then_inc(gates_read, 1)
                    dve.memset(credit3[:, 1:2], 0.0).then_inc(x1_ready, 1)
                    for i in range(2):
                        dve.memset(credit3[:, 3 + i:4 + i], 0.0).then_inc(g_split, 1)
                        dve.memset(credit3[:, 5 + i:6 + i], 0.0).then_inc(down_done, 1)
                    dve.wait_ge(rank_read, 1)
                    dve.wait_ge(wsmall_in, 16 * 5)
                    attention_sum(0, 0, 0, 16)
                    for n in range(2):
                        stage_low(dve, 0, n)
                    second_norm(0, 0, 0)
                    split_turned(0, 0)
                    with dve.Fori(0, NB // 2) as bb:
                        b = 2 * bb
                        at = (b + 1) * TPB
                        for f in range(FC):
                            split_hidden(b, f)
                            if f == 0:
                                attention_sum(b + 1, 1, at, 16 * (bb + 1))
                            elif f == 3:
                                second_norm(b + 1, 1, at)
                            if f in (2, 4, 6):
                                stage_low(dve, *beside(0, f // 2 - 1, bb))
                        split_turned(b + 1, 1)
                        new_x(b, bb, 0)
                        at = (b + 2) % NB * TPB
                        for f in range(FC):
                            split_hidden(b + 1, f)
                            if f == 0:
                                new_moments(0)
                            elif f == 1:
                                expert_rows_of(b, 0)
                            elif f == 2:
                                attention_sum(b + 2, 0, at, 16 * (bb + 2))
                            elif f == 4:
                                second_norm(b + 2, 0, at)
                            elif f == 5:
                                choose(b)
                            elif f == 7:
                                send(b)
                            if f in (2, 5):
                                stage_low(dve, *beside(1, f // 3, bb))
                        split_turned(b + 2, 0)
                        new_x(b + 1, bb, 1)
                        new_moments(1)
                        expert_rows_of(b + 1, 1)
                        stage_low(dve, *beside(1, 2, bb))
                        choose(b + 1)
                        send(b + 1)

                    steps = [0]

                    def then(ins):
                        steps[0] += 1
                        ins.then_inc(link_e, 1)
                        dve.wait_ge(link_e, steps[0])
                    cnt, up127 = nblk[:, 0, :], nblk[:, 1, :]
                    then(dve.tensor_tensor(cnt, place[:, :], region0[:, :], ALU.subtract))
                    then(dve.tensor_scalar(up127, cnt, float(P - 1), None, ALU.add))
                    then(dve.tensor_copy(counts[:, 0, :], cnt))
                    then(dve.tensor_copy(counts[:, 1, :], up127))
                    then(dve.tensor_scalar(counts[:, 2, :], counts[:, 1, :], P.bit_length() - 1, None,
                                           ALU.arith_shift_right))
                    then(dve.tensor_copy(nblk[:, 2, :], counts[:, 2, :]))
                    then(dve.tensor_copy(ends[:, 0:1], nblk[:, 2, 0:1]))
                    for e in range(1, E):
                        then(dve.tensor_tensor(ends[:, e:e + 1], ends[:, e - 1:e], nblk[:, 2, e:e + 1], ALU.add))
                    NJ = NBLK + 2
                    then(dve.tensor_tensor(past[:, 0, :, :], blocks[:, :].unsqueeze(2).to_broadcast([P, NJ, E]),
                                           ends[:, :].unsqueeze(1).to_broadcast([P, NJ, E]), ALU.is_ge))
                    then(dve.tensor_tensor(past[:, 1, :, :], past[:, 0, :, :],
                                           nblk[:, 2, :].unsqueeze(1).to_broadcast([P, NJ, E]), ALU.mult))
                    then(dve.tensor_reduce(tabf[:, 0:2, :], past[:, :, :, :], AX.X, ALU.add))
                    then(dve.tensor_tensor(tabf[:, 2, :], blocks[:, :], tabf[:, 1, :], ALU.subtract))
                    then(dve.tensor_scalar(tabf[:, 3, :], tabf[:, 0, :], float(REGION), None, ALU.mult))
                    then(dve.scalar_tensor_tensor(out=tabf[:, 4, :], in0=tabf[:, 2, :], scalar=float(P),
                                                  in1=tabf[:, 3, :], op0=ALU.mult, op1=ALU.add))
                    then(dve.tensor_scalar(table[:, 1, :], tabf[:, 4, :], float(E * REGION), None, ALU.min))
                    dve.tensor_scalar(table[:, 0, :], tabf[:, 0, :], float(E - 1), None, ALU.min)\
                        .then_inc(table_ready, 1)

                @block.scalar
                def _(act):
                    def high_turned(b, p):
                        for c in range(DC):
                            act.wait_ge(h2T_ready, DC * b + c + 1)
                            act.activation(hT[:, p, 0, c, :], ps[:, 2 + c, :], ACT.Copy).then_inc(h2T_high, 1)

                    def hidden_high(b, f):
                        act.wait_ge(g_split, FC * b + f + 1)
                        act.wait_ge(up_ready, FC * b + f + 1)
                        act.activation(g32[:, f % 2, :], ps[:, f % 2, :], ACT.Gelu_apprx_tanh,
                                       scale=1.0 / WSCALE).then_inc(gelu_ready, 1)
                        act.wait_ge(gelu_ready, FC * b + f + 1)
                        act.wait_ge(down_done, FC * b + f + 1)
                        act.activation(gT[:, 0, f % 2, :], g32[:, f % 2, :], ACT.Copy).then_inc(g_high, 1)

                    def copy_xnT(b):
                        act.wait_ge(xnT_ready, b + 1)
                        act.activation(xnT[:, :, :], ps[:, 2:4, :], ACT.Copy).then_inc(xnT_copied, 1)

                    def gap_exponential(b):
                        act.wait_ge(gap_ready, b + 1)
                        act.activation(gap[:, 1, :], gap[:, 0, :], ACT.Exp).then_inc(gap_exp, 1)

                    for n in range(2):
                        stage_high(act, 0, n)
                    high_turned(0, 0)
                    with act.Fori(0, NB // 2) as bb:
                        for p in range(2):
                            b = 2 * bb + p
                            for f in range(FC):
                                hidden_high(b, f)
                                if f in (1, 3, 5):
                                    stage_high(act, *beside(p, f // 2, bb))
                                if p and f == 4:
                                    copy_xnT(b - 1)
                                if p and f == 7:
                                    gap_exponential(b - 1)
                            high_turned(b + 1, 1 - p)
                        copy_xnT(b)
                        gap_exponential(b)

                @block.tensor
                def _(pe):
                    def attention_out(b):
                        pe.wait_ge(ctx_scaled, b + 1)
                        for a in range(TPB):
                            for c in range(DC):
                                mm = pe.matmul(ps[:, 2 + a // 2, a % 2 * D:(a % 2 + 1) * D],
                                               cT[:, c, a * P:(a + 1) * P], wo[:, c, :],
                                               start=(c == 0), stop=(c == DC - 1))
                            mm.then_inc(attn_ready, 1)

                    def turn_h2(b, p):
                        pe.wait_ge(h2_ready, TPB * b + TPB)
                        for c in range(DC):
                            for a in range(TPB):
                                mm = pe.transpose(ps[:, 2 + c, a * P:(a + 1) * P], htb[:, p, a, c * P:(c + 1) * P],
                                                  ident[:, :])
                            mm.then_inc(h2T_ready, 1)

                    def hidden(b, p, f):
                        if f >= 2:
                            pe.wait_ge(gelu_ready, FC * b + f - 1)
                        for n, (w, h) in enumerate(((0, 0), (0, 1), (1, 0))):
                            for c in range(DC):
                                mm = pe.matmul(ps[:, f % 2, :], up(0, w, c, f), hT[:, p, h, c, :],
                                               start=(n == 0 and c == 0), stop=(n == 2 and c == DC - 1))
                        mm.then_inc(up_ready, 1)

                    def back(b, f):
                        pe.wait_ge(g_split, FC * b + f + 3)
                        if f == 0:
                            pe.wait_ge(x1_ready, TPB * b + 1)
                        for a in range(TPB):
                            for n, (g, w) in enumerate(((0, 0), (0, 1), (1, 0))):
                                mm = pe.matmul(ps[:, 4 + a, 0:D], gT[:, g, f % 2, a * P:(a + 1) * P], down(0, w, f),
                                               start=(f == 0 and n == 0), stop=(f == FC - 1 and n == 2))
                        mm.then_inc(down_done, 1)

                    def turn_xn(b):
                        pe.wait_ge(xn_ready, TPB * b + TPB)
                        for c in range(DC):
                            for a in range(TPB):
                                mm = pe.transpose(ps[:, 2 + c, a * P:(a + 1) * P], rows[:, a, c * P:(c + 1) * P],
                                                  ident[:, :])
                        mm.then_inc(xnT_ready, 1)

                    def gates(b):
                        pe.wait_ge(xnT_copied, b + 1)
                        for a in range(TPB):
                            for c in range(DC):
                                mm = pe.matmul(ps[:, 2, a * E:(a + 1) * E], xnT[:, c, a * P:(a + 1) * P],
                                               gw[:, c, :], start=(c == 0), stop=(c == DC - 1))
                        mm.then_inc(gates_ready, 1)

                    def ranks(b):
                        pe.wait_ge(member_ready, b + 1)
                        for a in range(TPB):
                            for k in range(a + 1):
                                pe.matmul(ps[:, 3, a * E:(a + 1) * E], (before if k == a else onesb)[:, :],
                                          member[:, k, :], start=(k == 0), stop=(k == a))
                        for k in range(TPB):
                            mm = pe.matmul(ps[:, 3, TPB * E:(TPB + 1) * E], onesb[:, :], member[:, k, :],
                                           start=(k == 0), stop=(k == TPB - 1))
                        mm.then_inc(rank_ready, 1)

                    pe.wait_ge(wsmall_in, 16 * 5)
                    pe.wait_ge(c3_ready, 8)
                    attention_out(0)
                    turn_h2(0, 0)
                    for n in range(2):
                        pe.wait_ge(wst_split[n], 1)
                    with pe.Fori(0, NB // 2) as bb:
                        b = 2 * bb
                        pe.wait_ge(h2T_split, DC * (b + 1))
                        pe.wait_ge(gates_read, b + 1)
                        pe.wait_ge(rank_read, b + 1)
                        attention_out(b + 1)
                        hidden(b, 0, 0)
                        for f in range(FC):
                            if f + 1 < FC:
                                hidden(b, 0, f + 1)
                            back(b, f)
                            if f == 5:
                                turn_h2(b + 1, 1)
                        pe.wait_ge(h2T_split, DC * (b + 2))
                        attention_out(b + 2)
                        hidden(b + 1, 1, 0)
                        for f in range(FC):
                            if f + 1 < FC:
                                hidden(b + 1, 1, f + 1)
                            back(b + 1, f)
                            if f == 3:
                                pe.wait_ge(var3[0], b + 3)
                                turn_xn(b)
                            elif f == 4:
                                gates(b)
                            elif f == 6:
                                ranks(b)
                            elif f == 7:
                                pe.wait_ge(gates_read, b + 2)
                                pe.wait_ge(rank_read, b + 2)
                                turn_h2(b + 2, 0)
                        pe.wait_ge(h2T_split, DC * (b + 3))
                        turn_xn(b + 1)
                        gates(b + 1)
                        ranks(b + 1)

        ph4 = ExitStack()
        with ph4:
            def s4(name, shape, dt):
                return sb(name, shape, dt, ph4)
            xr = s4("xr", [P, 2, ROW], F32)
            meta = s4("meta", [P, 2, ROW - D], F32)
            xT = s4("xT", [P, 2, 2, D], F16)
            g4 = s4("g4", [P, 2, HE], F32)
            gT4 = s4("gT4", [P, 2, 2, HE], F16)
            y4 = s4("y4", [P, 2, D], F32)
            ids = s4("ids", [P, 2, 1], U32)
            credit4 = s4("credit4", [P, 2], F32)

            row_in = [sem("row_in0"), sem("row_in1")]
            xT_ready = sem("xT_ready")
            xT_high = sem("xT_high")
            xT_split = sem("xT_split")
            mid_ready = sem("mid_ready")
            mid_gelu = sem("mid_gelu")
            mid_high = sem("mid_high")
            mid_split = sem("mid_split")
            end_ready = sem("end_ready")
            y_step = sem("y_step")
            y_ready = sem("y_ready")
            meta_ready = sem("meta_ready")
            added = [sem("added0"), sem("added1")]
            out_done = sem("out_done")
            LATE = range(SPLIT3 + 1, SETS)

            def first_row(eng, j):
                return eng.value_load(table[0:1, 1, bass.ds(j, 1)], min_val=0, max_val=E * REGION)

            def expert(eng, j):
                return eng.value_load(table[0:1, 0, bass.ds(j, 1)], min_val=0, max_val=E - 1)

            block = nc.Block()
            with block:
                @block.sync
                def _(sp):
                    for q in range(2):
                        sp.dma_start(xr[:, q, :], expert_rows[bass.ds(first_row(sp, q), P), :]).then_inc(row_in[q], 16)
                    for s in LATE:
                        for n in range(2):
                            load_stage(sp, s, n)
                    with sp.Fori(0, NBLK // 2) as jj:
                        for q in range(2):
                            j = 2 * jj + q
                            sp.wait_ge(xT_ready, j + 1)
                            sp.wait_ge(meta_ready, j + 1)
                            sp.dma_start(xr[:, q, :], expert_rows[bass.ds(first_row(sp, j + 2), P), :])\
                                .then_inc(row_in[q], 16)
                    for q in range(2):
                        sp.wait_ge(added[q], 16 * (NBLK // 2 + 1))
                    sp.dma_start(out[:, :], sum_rows[0:T, :]).then_inc(out_done, 16)
                    sp.wait_ge(out_done, 16)
                    for q in range(2):
                        sp.wait_ge(row_in[q], 16 * (NBLK // 2 + 1))

                @block.gpsimd
                def _(pool):
                    for i in range(2):
                        pool.dma_start(sum_rows[T + i * (P // 2):T + (i + 1) * (P // 2), :],
                                       pad[i * (P // 2):(i + 1) * (P // 2), 0:D]).then_inc(added[i], 16)
                    with pool.Fori(0, NBLK // 2) as jj:
                        for q in range(2):
                            j = 2 * jj + q
                            pool.wait_ge(y_step, 2 * j + 2)
                            pool.wait_ge(y_ready, j + 3)
                            wait_apart(pool, added[1 - q], 16 * (jj + 1 + q))
                            pool.indirect_dma_start(
                                out=sum_rows[:, :], in_=y4[:, q, :], in_offset=None,
                                out_offset=bass.IndirectOffsetOnAxis(ap=ids[:, q, :], axis=0),
                                bounds_check=T + P - 1, compute_op=ALU.add).then_inc(added[q], 16)

                @block.vector
                def _(dve):
                    def low_rows(j, q):
                        dve.wait_ge(xT_high, j + 1)
                        dve.tensor_tensor(xT[:, q, 1, :], ps[:, 6 + q, 0:D], xT[:, q, 0, :], ALU.subtract)\
                            .then_inc(xT_split, 1)

                    def keep_meta(j, q, loads):
                        dve.wait_ge(row_in[q], loads)
                        dve.tensor_copy(meta[:, q, :], xr[:, q, D:ROW]).then_inc(meta_ready, 1)

                    def low_hidden(j, q):
                        dve.wait_ge(mid_high, j + 1)
                        dve.tensor_tensor(gT4[:, 1, q, :], g4[:, q, :], gT4[:, 0, q, :], ALU.subtract)\
                            .then_inc(mid_split, 1)

                    for i in range(2):
                        dve.memset(credit4[:, i:i + 1], 0.0).then_inc(y_ready, 1)
                    for q in range(2):
                        low_rows(q, q)
                        keep_meta(q, q, 16)
                    for n in range(2):
                        stage_low(dve, LATE[0], n)
                    low_hidden(0, 0)
                    for n in range(2):
                        stage_low(dve, LATE[1], n)
                    dve.wait_ge(c_in, 32)
                    with dve.Fori(0, NBLK // 2) as jj:
                        for q in range(2):
                            j = 2 * jj + q
                            low_rows(j + 2, q)
                            low_hidden(j + 1, 1 - q)
                            e = expert(dve, j)
                            dve.wait_ge(end_ready, j + 1)
                            dve.wait_ge(added[q], 16 * (jj + 1))
                            dve.scalar_tensor_tensor(out=y4[:, q, :], in0=ps[:, 4 + q, 0:D], scalar=1.0 / WSCALE,
                                                     in1=b2b[:, e, :], op0=ALU.mult, op1=ALU.add)\
                                .then_inc(y_step, 1)
                            dve.wait_ge(meta_ready, j + 1)
                            dve.tensor_copy(ids[:, q, :], meta[:, q, E:E + 1]).then_inc(y_step, 1)
                            dve.wait_ge(y_step, 2 * j + 2)
                            dve.tensor_scalar(y4[:, q, :], y4[:, q, :], meta[:, q, bass.ds(e, 1)], None, ALU.mult)\
                                .then_inc(y_ready, 1)
                            dve.wait_ge(y_ready, j + 3)
                            keep_meta(j + 2, q, 16 * (jj + 2))

                @block.scalar
                def _(act):
                    def high_rows(j, q):
                        act.wait_ge(xT_ready, j + 1)
                        act.activation(xT[:, q, 0, :], ps[:, 6 + q, 0:D], ACT.Copy).then_inc(xT_high, 1)

                    def middle(j, q):
                        e = expert(act, j)
                        for m in range(HC):
                            if m % 4 == 0:
                                act.wait_ge(mid_ready, 2 * j + m // 4 + 1)
                            act.activation(g4[:, q, m * P:(m + 1) * P],
                                           ps[:, 2 * q + m // 4, m % 4 * P:(m % 4 + 1) * P], ACT.Gelu,
                                           bias=b1s[:, e, m:m + 1], scale=1.0 / WSCALE).then_inc(mid_gelu, 1)
                        act.wait_ge(mid_gelu, HC * j + HC)
                        act.activation(gT4[:, 0, q, :], g4[:, q, :], ACT.Copy).then_inc(mid_high, 1)

                    for n in range(2):
                        stage_high(act, LATE[0], n)
                    act.wait_ge(c_in, 32)
                    for q in range(2):
                        high_rows(q, q)
                    middle(0, 0)
                    for n in range(2):
                        stage_high(act, LATE[1], n)
                    with act.Fori(0, NBLK // 2) as jj:
                        for q in range(2):
                            j = 2 * jj + q
                            high_rows(j + 2, q)
                            middle(j + 1, 1 - q)

                @block.tensor
                def _(pe):
                    def turn_rows(j, q, loads):
                        pe.wait_ge(row_in[q], loads)
                        for c in range(DC):
                            mm = pe.transpose(ps[:, 6 + q, c * P:(c + 1) * P], xr[:, q, c * P:(c + 1) * P],
                                              ident[:, :])
                        mm.then_inc(xT_ready, 1)

                    def first_half(j, q, e):
                        s = e + 1
                        for n in range(2):
                            pe.wait_ge(wst_split[n], s + 1)
                        pe.wait_ge(xT_split, j + 1)
                        for m in range(HC):
                            for c in range(DC):
                                for n, (w, x_) in enumerate(((0, 0), (0, 1), (1, 0))):
                                    mm = pe.matmul(ps[:, 2 * q + m // 4, m % 4 * P:(m % 4 + 1) * P],
                                                   up(s, w, c, m), xT[:, q, x_, c * P:(c + 1) * P],
                                                   start=(n == 0 and c == 0), stop=(n == 2 and c == DC - 1))
                            if m % 4 == 3:
                                mm.then_inc(mid_ready, 1)

                    def second_half(j, q, e):
                        s = e + 1
                        pe.wait_ge(mid_split, j + 1)
                        pe.wait_ge(y_ready, j + 1)
                        for m in range(HC):
                            for n, (g, w) in enumerate(((0, 0), (0, 1), (1, 0))):
                                mm = pe.matmul(ps[:, 4 + q, 0:D], gT4[:, g, q, m * P:(m + 1) * P], down(s, w, m),
                                               start=(m == 0 and n == 0), stop=(m == HC - 1 and n == 2))
                        mm.then_inc(end_ready, 1)

                    for q in range(2):
                        turn_rows(q, q, 16)
                    first_half(0, 0, expert(pe, 0))
                    with pe.Fori(0, NBLK // 2) as jj:
                        j = 2 * jj
                        this, following = expert(pe, j), expert(pe, j + 1)
                        turn_rows(j + 2, 0, 16 * (jj + 2))
                        first_half(j + 1, 1, following)
                        second_half(j, 0, this)
                        after = expert(pe, j + 2)
                        turn_rows(j + 3, 1, 16 * (jj + 2))
                        first_half(j + 2, 0, after)
                        second_half(j + 1, 1, following)


_ORDER = ["x", "adj", "adjT", "nodemask", "L0_gnn_h_target", "L0_gnn_ln1_scale", "L0_gnn_ln1_bias", "L0_gnn_Wq",
          "L0_gnn_bq", "L0_gnn_Wk", "L0_gnn_bk", "L0_gnn_Wv", "L0_gnn_bv", "L0_gnn_Wo", "L0_gnn_bo",
          "L0_gnn_ln2_scale", "L0_gnn_ln2_bias", "L0_gnn_W1", "L0_gnn_W2", "gate_wT", "w1T", "L0_ffn_b1", "w2T",
          "L0_ffn_b2"]


def layout(**inputs):
    import numpy as np

    a = {k: np.ascontiguousarray(v) for k, v in inputs.items()}
    a["adjT"] = np.ascontiguousarray(a["adj"].T)
    a["gate_wT"] = np.ascontiguousarray(a.pop("L0_ffn_gate_w").T)
    a["w1T"] = np.ascontiguousarray(a.pop("L0_ffn_w1").transpose(0, 2, 1))
    a["w2T"] = np.ascontiguousarray(a.pop("L0_ffn_w2").transpose(0, 2, 1))
    b1 = a["L0_ffn_b1"]
    a["L0_ffn_b1"] = np.ascontiguousarray(b1.reshape(b1.shape[0], -1, 128).transpose(2, 0, 1))
    return {f"in_{k}": a[k] for k in _ORDER}


def declare(nc, arrays):
    args = [nc.dram_tensor(k, a.shape, mybir.dt.from_np(a.dtype), kind="ExternalInput").ap()
            for k, a in arrays.items()]
    shape = arrays["in_x"].shape
    return args + [nc.dram_tensor("out_rows", shape, F32, kind="ExternalOutput").ap()]


def kernel(**inputs):
    import concourse.bacc as bacc
    from concourse.bass_utils import run_bass_kernel_spmd

    arrays = layout(**inputs)
    nc = bacc.Bacc("TRN2", target_bir_lowering=False, num_devices=1)
    graph_attention_and_experts(nc, *declare(nc, arrays))
    return run_bass_kernel_spmd(nc, [arrays], core_ids=[0]).results[0]["out_rows"]
```

```python
from contextlib import ExitStack

import concourse.bass as bass
from concourse import mybir

ALU = mybir.AluOpType
ACT = mybir.ActivationFunctionType
AX = mybir.AxisListType
F32 = mybir.dt.float32
F32R = mybir.dt.float32r
BF16 = mybir.dt.bfloat16
F16 = mybir.dt.float16
I32 = mybir.dt.int32
U32 = mybir.dt.uint32

P = 128
EPS = 1e-5
NO_EDGE = -(2.0**100)
WSCALE = 64.0


def at_least(eng, sem, value):
    if not isinstance(value, int) or value > 0:
        eng.wait_ge(sem, value)


def graph_attention_and_experts(nc, x, adj, adjT, nodemask, h_target, ln1_scale, ln1_bias, Wq, bq, Wk, bk, Wv, bv,
                                Wo, bo, ln2_scale, ln2_bias, W1, W2, gate_wT, w1T, b1, w2T, b2, out):
    T, D = x.shape
    NT = T // P
    DC = D // P
    H = 8
    HD = D // H
    TB = 512
    NB = T // TB
    TPB = TB // P
    GT = 4
    NG = NT // GT
    QSCALE = float(HD) ** -0.5
    KR = 3 * HD
    F = W1.shape[1]
    FC = F // P
    E, _, HE = w1T.shape
    HC = HE // P

    ctx = ExitStack()
    with ctx:
        def sem(name):
            return ctx.enter_context(nc.semaphore(name))

        def sb(name, shape, dt, scope=ctx):
            return scope.enter_context(nc.sbuf_tensor(name, shape, dt))

        def dram(name, shape, dt):
            return nc.dram_tensor(name, shape, dt).ap()

        k_stack = dram("k_stack", [H, 3, HD, T], F32)
        q_stack = dram("q_stack", [H, 3, HD, T], F32)
        ht_rows = dram("ht_rows", [T, D], F32)
        ctx_cols = dram("ctx_cols", [D, T], F32)
        sums = dram("sums", [P, NB * H + 1, TPB], F32)
        inv_sums = dram("inv_sums", [NB * H * TPB, P], F32)

        ps = ctx.enter_context(nc.psum_tensor("ps", [P, 8, 512], F32))
        ident = sb("ident", [P, P], F32)
        identb = sb("identb", [P, P], BF16)
        m01 = sb("m01", [P, NT], F32)
        minus_half = sb("minus_half", [P, NT], F32)

        const_ready = sem("const_ready")

        def wait_apart(eng, signal, value):
            if not isinstance(value, int):
                value = eng.to_reg(value)
            eng.wait_ge(const_ready, 3)
            eng.wait_ge(signal, value)

        ph1 = ExitStack()
        ph12 = ExitStack()
        ctx.enter_context(ph12)
        v_all = sb("v_all", [P, NT, D], F32, ph12)

        x_in = sem("x_in")
        h_in = sem("h_in")
        small_in = sem("small_in")
        w_in = sem("w_in")
        stat_step = sem("stat_step")
        var_ready = sem("var_ready")
        rstd_ready = sem("rstd_ready")
        dve_step = sem("dve_step")
        xn_ready1 = sem("xn_ready1")
        xn_scaled = sem("xn_scaled")
        hn_ready = sem("hn_ready")
        hn_scaled = sem("hn_scaled")
        hs_ready = sem("hs_ready")
        ht_ready = sem("ht_ready")
        tr_ready = sem("tr_ready")
        tr_copied = sem("tr_copied")
        kq_ready = sem("kq_ready")
        kq_high = sem("kq_high")
        kq_split = sem("kq_split")
        v_ready = sem("v_ready")
        v_stored = sem("v_stored")
        kq_out = [sem("kq_out0"), sem("kq_out1")]
        ht_out = sem("ht_out")
        wq_scaled = sem("wq_scaled")
        pool_step = sem("pool_step")

        with ph1:
            def s1(name, shape, dt):
                return sb(name, shape, dt, ph1)
            xs = s1("xs", [P, NT, D], F32)
            hh = s1("hh", [P, NT, D], F32)
            sT = s1("sT", [P, 2, DC, GT * P], F32)
            kq_hi = s1("kq_hi", [P, 2, 512], F32R)
            kq_lo = s1("kq_lo", [P, 2, 512], F32R)
            wqkv = s1("wqkv", [P, 3, DC, D], F32)
            ln_s = s1("ln_s", [P, D], F32)
            ln_b = s1("ln_b", [P, D], F32)
            bv_b = s1("bv_b", [P, D], F32)
            bkq = s1("bkq", [P, 2, DC], F32)
            nm_i = s1("nm_i", [P, NT], I32)
            stats = s1("stats", [P, 3, NT, 6], F32)
            mean = s1("mean", [P, 3, NT], F32)
            var = s1("var", [P, 3, NT], F32)
            rstd = s1("rstd", [P, 3, NT], F32)
            tmp = s1("tmp", [P, 4, NT], F32)

            block = nc.Block()
            with block:
                @block.sync
                def _(sp):
                    sp.dma_start(xs[:, :, :], x.rearrange("(i p) d -> p i d", p=P)).then_inc(x_in, 16)
                    sp.dma_start(hh[:, :, :], h_target.rearrange("(i p) d -> p i d", p=P)).then_inc(h_in, 16)
                    sp.dma_start(ln_s[:, :], ln1_scale.partition_broadcast(P)).then_inc(small_in, 16)
                    sp.dma_start(ln_b[:, :], ln1_bias.partition_broadcast(P)).then_inc(small_in, 16)
                    sp.dma_start(nm_i[:, :], nodemask.rearrange("(i p) -> p i", p=P),
                                 allow_slow_non_contiguous=True).then_inc(small_in, 16)
                    sp.dma_start(bv_b[:, :], bv.partition_broadcast(P)).then_inc(small_in, 16)
                    for n, w in enumerate((Wk, Wq, Wv)):
                        sp.dma_start(wqkv[:, n, :, :], w.rearrange("(c p) n -> p c n", p=P)).then_inc(w_in, 16)
                    for n, w in enumerate((bk, bq)):
                        sp.dma_start(bkq[:, n, :], w.rearrange("(c p) -> p c", p=P),
                                     allow_slow_non_contiguous=True).then_inc(w_in, 16)
                    for n, stack in enumerate((k_stack, q_stack)):
                        with sp.Fori(0, NG) as g:
                            for c in range(DC):
                                sp.wait_ge(kq_split, n * NG * DC + DC * g + c + 1)
                                for r, part in enumerate((kq_hi, kq_lo, kq_hi) if n == 0 else (kq_hi, kq_hi, kq_lo)):
                                    sp.dma_start(stack[4 * c:4 * c + 4, r, :, bass.ds(g * 512, 512)],
                                                 part[:, c, :].bitcast(F32))\
                                        .then_inc(kq_out[c], 16)
                    sp.wait_ge(ht_ready, NT)
                    sp.dma_start(ht_rows.rearrange("(i p) d -> p i d", p=P), hh[:, :, :]).then_inc(ht_out, 16)
                    sp.wait_ge(ht_out, 16)
                    for c in range(DC):
                        sp.wait_ge(kq_out[c], 2 * NG * 3 * 16)

                @block.gpsimd
                def _(pool):
                    pool.memset(minus_half[:, :], -0.5).then_inc(const_ready, 1)
                    pool.memset(ident[:, :], 0.0).then_inc(pool_step, 1)
                    pool.memset(identb[:, :], 0.0).then_inc(pool_step, 1)
                    pool.wait_ge(pool_step, 2)
                    for m in (ident, identb):
                        pool.affine_select(out=m[:, :], in_=m[:, :], compare_op=ALU.not_equal, fill=1.0, base=0,
                                           pattern=[[-1, P]], channel_multiplier=1).then_inc(const_ready, 1)
                    pool.wait_ge(const_ready, 1)
                    def inverse_root(n, turn):
                        pool.wait_ge(var_ready, turn)
                        pool.tensor_tensor(rstd[:, n, :], var[:, n, :], minus_half[:, :], ALU.pow)\
                            .then_inc(rstd_ready, 1)

                    def scale_rows(rows, normalised, scaled):
                        for i in range(NT):
                            pool.wait_ge(normalised, i + 1)
                            pool.tensor_tensor(rows[:, i, :], rows[:, i, :], ln_s[:, :], ALU.mult).then_inc(scaled, 1)

                    inverse_root(0, 1)
                    inverse_root(2, 2)
                    pool.wait_ge(small_in, 64)
                    scale_rows(xs, xn_ready1, xn_scaled)
                    inverse_root(1, 3)
                    scale_rows(hh, hn_ready, hn_scaled)

                @block.vector
                def _(dve):
                    steps = [0]

                    def then(ins):
                        steps[0] += 1
                        ins.then_inc(stat_step, 1)
                        dve.wait_ge(stat_step, steps[0])

                    def moments(n):
                        e, o = stats[:, n, :, 1], stats[:, n, :, 4]
                        dve.tensor_tensor(tmp[:, 0, :], e, o, ALU.add)
                        dve.tensor_tensor(tmp[:, 1, :], e, o, ALU.subtract)
                        then(dve.tensor_tensor(tmp[:, 2, :], stats[:, n, :, 2], stats[:, n, :, 5], ALU.add))
                        dve.tensor_scalar(mean[:, n, :], tmp[:, 0, :], 0.5, None, ALU.mult)
                        then(dve.tensor_tensor(tmp[:, 3, :], tmp[:, 1, :], tmp[:, 1, :], ALU.mult))
                        then(dve.tensor_scalar(tmp[:, 3, :], tmp[:, 3, :], 0.25, EPS, ALU.mult, ALU.add))
                        dve.scalar_tensor_tensor(out=var[:, n, :], in0=tmp[:, 2, :], scalar=1.0 / D, in1=tmp[:, 3, :],
                                                 op0=ALU.mult, op1=ALU.add).then_inc(var_ready, 1)

                    def tile_stats(n, src, done):
                        for i in range(NT):
                            dve.bn_stats(stats[:, n, i, :], src[:, i, :]).then_inc(dve_step, 1)
                        dve.wait_ge(dve_step, done)
                        moments(n)

                    def normalise(n, rows, done):
                        for i in range(NT):
                            dve.tensor_scalar(rows[:, i, :], rows[:, i, :], mean[:, n, i:i + 1],
                                              rstd[:, n, i:i + 1], ALU.subtract, ALU.mult).then_inc(done, 1)

                    def shift(rows, scaled, done):
                        for i in range(NT):
                            dve.wait_ge(scaled, i + 1)
                            dve.scalar_tensor_tensor(out=rows[:, i, :], in0=ln_b[:, :], scalar=m01[:, i:i + 1],
                                                     in1=rows[:, i, :], op0=ALU.mult, op1=ALU.add).then_inc(done, 1)

                    dve.wait_ge(x_in, 16)
                    tile_stats(0, xs, NT)
                    dve.wait_ge(small_in, 64)
                    then(dve.tensor_scalar(m01[:, :], nm_i[:, :], 1.0, None, ALU.is_equal))
                    dve.wait_ge(rstd_ready, 1)
                    for i in range(NT):
                        dve.tensor_scalar(xs[:, i, :], xs[:, i, :], mean[:, 0, i:i + 1], rstd[:, 0, i:i + 1],
                                          ALU.subtract, ALU.mult).then_inc(dve_step, 1)
                        dve.wait_ge(dve_step, NT + 2 * i + 1)
                        dve.bn_stats(stats[:, 2, i, :], xs[:, i, :]).then_inc(dve_step, 1)
                    dve.wait_ge(dve_step, 3 * NT)
                    moments(2)
                    dve.wait_ge(w_in, 16 * 5)
                    dve.tensor_scalar(wqkv[:, 1, :, :], wqkv[:, 1, :, :], QSCALE, None, ALU.mult)\
                        .then_inc(wq_scaled, 1)
                    dve.tensor_scalar(bkq[:, 1, :], bkq[:, 1, :], QSCALE, None, ALU.mult)\
                        .then_inc(wq_scaled, 1)
                    dve.wait_ge(rstd_ready, 2)
                    then(dve.tensor_tensor(rstd[:, 2, :], rstd[:, 2, :], m01[:, :], ALU.mult))
                    normalise(2, xs, xn_ready1)
                    dve.wait_ge(h_in, 16)
                    tile_stats(1, hh, 4 * NT)
                    shift(xs, xn_scaled, hs_ready)
                    dve.wait_ge(rstd_ready, 3)
                    then(dve.tensor_tensor(rstd[:, 1, :], rstd[:, 1, :], m01[:, :], ALU.mult))
                    normalise(1, hh, hn_ready)

                    def split_low(n, g):
                        for c in range(DC):
                            k = n * NG * DC + DC * g + c
                            dve.wait_ge(kq_high, k + 1)
                            dve.scalar_tensor_tensor(out=kq_lo[:, c, :], in0=ps[:, 2 + c, :], scalar=bkq[:, n, c:c + 1],
                                                     in1=kq_hi[:, c, :].bitcast(F32), op0=ALU.add, op1=ALU.subtract)\
                                .then_inc(kq_split, 1)

                    with dve.Fori(0, NG) as g:
                        split_low(0, g)
                        for i in range(GT):
                            dve.wait_ge(v_ready, GT * g + i + 1)
                            dve.tensor_tensor(v_all[:, GT * g + i, :], ps[:, 4 + i, 0:D], bv_b[:, :], ALU.add)\
                                .then_inc(v_stored, 1)
                    shift(hh, hn_scaled, ht_ready)
                    with dve.Fori(0, NG) as g:
                        split_low(1, g)

                @block.scalar
                def _(act):
                    act.wait_ge(w_in, 16 * 5)

                    def copy_turned(k):
                        act.wait_ge(tr_ready, k + 1)
                        act.activation(sT[:, k % 2, :, :], ps[:, 0:2, :], ACT.Copy).then_inc(tr_copied, 1)

                    copy_turned(0)
                    for k in range(2 * NG):
                        n = k // NG
                        if k == NG:
                            act.wait_ge(wq_scaled, 2)
                        if k + 1 < NG:
                            copy_turned(k + 1)
                        for c in range(DC):
                            act.wait_ge(kq_ready, DC * k + c + 1)
                            at_least(act, kq_out[c], 48 * k)
                            act.activation(kq_hi[:, c, :], ps[:, 2 + c, :], ACT.Identity, bias=bkq[:, n, c:c + 1])\
                                .then_inc(kq_high, 1)
                        if NG <= k + 1 < 2 * NG:
                            copy_turned(k + 1)

                @block.tensor
                def _(pe):
                    pe.wait_ge(const_ready, 3)
                    pe.wait_ge(w_in, 16 * 5)

                    def turn(k):
                        n, g = k // NG, k % NG
                        src, ready = ((xs, hs_ready), (hh, ht_ready))[n]
                        at_least(pe, tr_copied, k)
                        for i in range(GT):
                            pe.wait_ge(ready, GT * g + i + 1)
                            for c in range(DC):
                                mm = pe.transpose(ps[:, c, i * P:(i + 1) * P],
                                                  src[:, GT * g + i, c * P:(c + 1) * P], ident[:, :])
                        mm.then_inc(tr_ready, 1)

                    def project(k):
                        for c in range(DC):
                            at_least(pe, kq_split, DC * (k - 1) + c + 1 if k else 0)
                            for j in range(DC):
                                mm = pe.matmul(ps[:, 2 + c, :], wqkv[:, k // NG, j, c * P:(c + 1) * P],
                                               sT[:, k % 2, j, :], start=(j == 0), stop=(j == DC - 1))
                            mm.then_inc(kq_ready, 1)

                    def values(g):
                        for i in range(GT):
                            at_least(pe, v_stored, GT * (g - 1) + i + 1 if g else 0)
                            for j in range(DC):
                                mm = pe.matmul(ps[:, 4 + i, 0:D], sT[:, g % 2, j, i * P:(i + 1) * P],
                                               wqkv[:, 2, j, :], start=(j == 0), stop=(j == DC - 1))
                            mm.then_inc(v_ready, 1)

                    turn(0)
                    for k in range(2 * NG):
                        if k == NG:
                            pe.wait_ge(wq_scaled, 2)
                        pe.wait_ge(tr_copied, k + 1)
                        if k + 1 < NG:
                            turn(k + 1)
                        project(k)
                        if k < NG:
                            values(k)
                        if NG <= k + 1 < 2 * NG:
                            turn(k + 1)

        UNITS = TPB * T // 512
        UPT = T // 512
        maxima_scores = sem("maxima_scores")
        maxima_read = sem("maxima_read")
        negmax_ready = sem("negmax_ready")
        rowsum_ready = sem("rowsum_ready")
        sums_out = [sem(f"sums_out{i}") for i in range(4)]
        negmax_turned = sem("negmax_turned")
        shift_high = sem("shift_high")
        shift_split = sem("shift_split")
        shift_rows = [sem(f"shift_rows{i}") for i in range(4)]
        q_in = [sem(f"q_in{i}") for i in range(4)]
        k_in = [sem(f"k_in{i}") for i in range(H)]
        scores_ready = sem("scores_ready")
        weights_ready = sem("weights_ready")
        context_added = sem("context_added")
        part_ready = sem("part_ready")
        context_summed = sem("context_summed")
        context_out = [sem(f"context_out{i}") for i in range(2)]
        maskA_ready = sem("maskA_ready")
        maskB_ready = sem("maskB_ready")
        adjA_in = [sem(f"adjA_in{i}") for i in range(2)]
        adjB_in = [sem(f"adjB_in{i}") for i in range(2)]
        ones_ready = sem("ones_ready")

        ph2 = ExitStack()
        with ph2:
            def s2(name, shape, dt):
                return sb(name, shape, dt, ph2)
            ks = s2("ks", [KR + 2, H, T], F32R)
            qs = s2("qs", [KR + 2, 4, TB], F32R)
            maskA = s2("maskA", [P, TPB, T], BF16)
            maskB = s2("maskB", [P, 2, NT, TB], BF16)
            adjA = s2("adjA", [P, 2, T], I32)
            adjB = s2("adjB", [P, 2, 2, TB], I32)
            weights = s2("weights", [P, 2, 2, TB], F32)
            masked = s2("masked", [P, 2, T], F32)
            rowsum = s2("rowsum", [P, 4, TPB], F32)
            piecemax = s2("piecemax", [P, 2, TPB, UPT], F32)
            negmax = s2("negmax", [P, 2, TPB], F32)
            shift_hi = s2("shift_hi", [TPB, 2, P], F32R)
            shift_lo = s2("shift_lo", [TPB, 2, P], F32R)
            credit = s2("credit", [P, 10], F32)
            part = s2("part", [2 * HD, TB // 2], F32)
            total = s2("total", [2 * HD, 2, TB // 2], F32)

            adj_t = adj.rearrange("(i p) s -> i p s", p=P)
            adjT_t = adjT.rearrange("(i p) t -> p i t", p=P)
            q_rows = q_stack.rearrange("h r d t -> h (r d) t")
            k_rows = k_stack.rearrange("h r d t -> h (r d) t")
            ctx_out = ctx_cols.rearrange("(h d) t -> h d t", d=HD)

            block = nc.Block()
            with block:
                @block.sync
                def _(sp):
                    def load_q(n, b, h):
                        sp.dma_start(qs[0:KR, h % 4, :].bitcast(F32), q_rows[h, :, bass.ds(b * TB, TB)])\
                            .then_inc(q_in[h % 4], 16)

                    def load_adjA(tile, a):
                        sp.dma_start(adjA[:, a % 2, :], adj_t[tile, :, :]).then_inc(adjA_in[a % 2], 16)

                    def load_adjB(b, h):
                        sp.dma_start(adjB[:, h % 2, :, :], adjT_t[:, 2 * h:2 * h + 2, bass.ds(b * TB, TB)])\
                            .then_inc(adjB_in[h % 2], 16)

                    def store_shift(n, h):
                        sp.wait_ge(shift_split, n + 1)
                        for r, rows in enumerate((shift_hi, shift_lo)):
                            sp.dma_start(qs[KR + r:KR + r + 1, h % 4, :].bitcast(F32), rows[:, h % 2, :].bitcast(F32))\
                                .then_inc(shift_rows[h % 4], 16)

                    def store_context(n, b, h):
                        wait_apart(sp, context_summed, n + 2)
                        for half in range(2):
                            sp.dma_start(ctx_out[h, :, bass.ds(b * TB + half * (TB // 2), TB // 2)],
                                         total[half * HD:(half + 1) * HD, h % 2, :])\
                                .then_inc(context_out[h % 2], 16)

                    def store_sums(n, h):
                        wait_apart(sp, rowsum_ready, TPB * (n + 1))
                        sp.dma_start(sums[:, bass.ds(n, 1), :], rowsum[:, h % 4, :]).then_inc(sums_out[h % 4], 16)

                    load_adjA(0, 0)
                    load_q(0, 0, 0)
                    sp.dma_start(ks[0:KR, 0, :].bitcast(F32), k_rows[0, :, :]).then_inc(k_in[0], 16)
                    load_adjA(1, 1)
                    for h in range(1, 3):
                        load_q(h, 0, h)
                        sp.dma_start(ks[0:KR, h, :].bitcast(F32), k_rows[h, :, :]).then_inc(k_in[h], 16)
                    for a in range(2, TPB):
                        sp.wait_ge(maskA_ready, a - 1)
                        load_adjA(a, a)
                    for h in range(2):
                        load_adjB(0, h)
                    store_shift(0, 0)
                    store_sums(0, 0)
                    for h in range(2, H):
                        sp.wait_ge(maskB_ready, h - 1)
                        load_adjB(0, h)
                    for h in range(3, H):
                        sp.dma_start(ks[0:KR, h, :].bitcast(F32), k_rows[h, :, :]).then_inc(k_in[h], 16)
                    with sp.Fori(0, NB) as b:
                        nxt = (b + 1) % NB
                        for h in range(H):
                            n = b * H + h
                            sp.wait_ge(scores_ready, n * 8 + 1)
                            load_q(n + 3, b if h + 3 < H else nxt, (h + 3) % H)
                            sp.wait_ge(maskB_ready, H + n - 1)
                            load_adjB(nxt, h)
                            if h in (H - 4, H - 3):
                                for a in range(2 * (h - H + 4), 2 * (h - H + 5)):
                                    sp.wait_ge(maskA_ready, TPB * (b + 1) + a - 1)
                                    load_adjA(nxt * TPB + a, a)
                            if h:
                                store_context(n - 1, b, h - 1)
                            store_sums(n + 1, (h + 1) % H)
                            store_shift(n + 1, (h + 1) % H)
                            if h == H - 1:
                                store_context(n, b, h)
                    for i in range(2):
                        sp.wait_ge(context_out[i], 16 + 32 * NB * H // 2)
                    for i in range(4):
                        sp.wait_ge(sums_out[i], 16 * (NB * H // 4 + (2 if i == 0 else 1)))
                        sp.wait_ge(q_in[i], 16 * (NB * H // 4 + (1 if i < 3 else 0)))
                        sp.wait_ge(shift_rows[i], 32 * (NB * H // 4 + (1 if i == 0 else 0)))
                    for i in range(2):
                        sp.wait_ge(adjA_in[i], 16 * (NB + 1) * TPB // 2)
                        sp.wait_ge(adjB_in[i], 16 * (NB + 1) * H // 2)

                @block.gpsimd
                def _(pool):
                    pool.memset(ks[KR:KR + 2, :, :].bitcast(F32), 1.0).then_inc(ones_ready, 1)

                @block.vector
                def _(dve):
                    dve.memset(credit[:, 0:1], 0.0).then_inc(context_summed, 1)
                    for i in range(4):
                        dve.memset(credit[:, 6 + i:7 + i], 0.0).then_inc(sums_out[i], 16)
                    for i in range(2):
                        dve.memset(credit[:, 1 + i:2 + i], 0.0).then_inc(context_added, 1)
                        dve.memset(credit[:, 3 + i:4 + i], 0.0).then_inc(context_out[i], 16)

                    def mask_a(b, a):
                        dve.wait_ge(adjA_in[a % 2], 16 * (b * (TPB // 2) + a // 2 + 1))
                        dve.tensor_scalar(maskA[:, a, :], adjA[:, a % 2, :], 0.0, NO_EDGE, ALU.is_equal, ALU.mult)\
                            .then_inc(maskA_ready, 1)

                    def mask_b(b, h):
                        dve.wait_ge(adjB_in[h % 2], 16 * (b * (H // 2) + h // 2 + 1))
                        dve.tensor_scalar(maskB[:, b % 2, 2 * h:2 * h + 2, :], adjB[:, h % 2, :, :], 0.0, NO_EDGE,
                                          ALU.is_equal, ALU.mult).then_inc(maskB_ready, 1)

                    def turned_shift(n, par):
                        dve.wait_ge(negmax_turned, n + 1)
                        turned = ps[0:TPB, 6 + par, 0:P]
                        dve.tensor_copy(shift_hi[:, par, :], turned).then_inc(shift_high, 1)
                        dve.wait_ge(shift_high, n + 1)
                        dve.tensor_tensor(shift_lo[:, par, :], turned, shift_hi[:, par, :].bitcast(F32),
                                          ALU.subtract).then_inc(shift_split, 1)

                    def add_halves(n, b, h):
                        dve.wait_ge(context_out[h % 2], 16 + 32 * (b * (H // 2) + h // 2))
                        dve.wait_ge(part_ready, n + 1)
                        dve.tensor_tensor(total[:, h % 2, :], ps[0:2 * HD, 6 + h % 2, 0:TB // 2],
                                          part[:, :], ALU.add)\
                            .then_inc(context_summed, 1)

                    def maxima(n, par, beside):
                        for u in range(UNITS):
                            a, k = u // UPT, u % UPT
                            if k == 0:
                                at_least(dve, rowsum_ready, TPB * n + a - 1)
                            wait_apart(dve, maxima_scores, UNITS * n + u + 1)
                            dve.tensor_tensor_reduce(masked[:, a % 2, k * 512:(k + 1) * 512], ps[:, u % 2, :],
                                                     maskA[:, a, k * 512:(k + 1) * 512],
                                                     1.0, NO_EDGE, ALU.add, ALU.max,
                                                     piecemax[:, par, a, k:k + 1]).then_inc(maxima_read, 1)
                            if k == UPT - 1:
                                dve.wait_ge(maxima_read, UNITS * n + u + 1)
                                dve.tensor_reduce(negmax[:, par, a:a + 1], piecemax[:, par, a, :], AX.X, ALU.max,
                                                  negate=True).then_inc(negmax_ready, 1)
                            beside(u)

                    def step(n, b, h):
                        def beside(u):
                            if u == 3 and h:
                                add_halves(n - 1, b, h - 1)
                            elif u == 5:
                                dve.wait_ge(scores_ready, 8 * H * b + 1)
                                mask_b(b + 1, h)
                            elif u == 9:
                                turned_shift(n + 1, (h + 1) % 2)
                            if h == H - 3 and u % UPT == UPT - 1:
                                mask_a(b + 1, u // UPT)
                        if h == H - 2:
                            dve.wait_ge(maskA_ready, TPB * (b + 2))
                        maxima(n + 2, h % 2, beside)
                        if h == H - 1:
                            add_halves(n, b, h)

                    def mask_next_tile(u):
                        a = u // UPT + 1
                        if u % UPT == UPT - 1 and a < TPB:
                            mask_a(0, a)
                            dve.wait_ge(maskA_ready, a + 1)

                    mask_a(0, 0)
                    dve.wait_ge(maskA_ready, 1)
                    maxima(0, 0, mask_next_tile)
                    turned_shift(0, 0)
                    maxima(1, 1, lambda u: None)
                    for h in range(H):
                        mask_b(0, h)
                    with dve.Fori(0, NB) as b:
                        for h in range(H):
                            step(b * H + h, b, h)

                @block.scalar
                def _(act):
                    def row_sums(n, b, h, a):
                        if a == 0:
                            act.wait_ge(sums_out[h % 4], 16 * (b * (H // 4) + h // 4 + 1))
                        act.wait_ge(negmax_ready, TPB * n + a + 1)
                        act.activation(masked[:, a % 2, :], masked[:, a % 2, :], ACT.Exp,
                                       bias=negmax[:, h % 2, a:a + 1],
                                       accum_out=rowsum[:, h % 4, a:a + 1]).then_inc(rowsum_ready, 1)

                    def copy_half(n, h):
                        act.wait_ge(context_added, 8 * n + 10)
                        act.wait_ge(context_summed, n + 1)
                        act.activation(part[:, :], ps[2 * HD:4 * HD, 6 + h % 2, 0:TB // 2], ACT.Copy).then_inc(part_ready, 1)

                    for a in range(TPB):
                        row_sums(0, 0, 0, a)
                    for a in range(TPB - 1):
                        row_sums(1, 0, 1, a)
                    act.wait_ge(ones_ready, 1)
                    act.activation(credit[0:2, 5:6], ks[KR:KR + 2, 0, 0:1].bitcast(F32), ACT.Copy)\
                        .then_inc(weights_ready, 1)
                    with act.Fori(0, NB) as b:
                        for h in range(H):
                            n = b * H + h
                            for j in range(8):
                                act.wait_ge(scores_ready, 8 * n + j + 1)
                                act.wait_ge(context_added, 8 * n + j + 1)
                                act.activation(weights[:, j % 2, :, :], ps[:, 2 + 2 * (j % 2):4 + 2 * (j % 2), :],
                                               ACT.Exp).then_inc(weights_ready, 1)
                                if j == 0:
                                    if h:
                                        copy_half(n - 1, h - 1)
                                    b1_, h1 = (b, h + 1) if h + 1 < H else (b + 1, 0)
                                    row_sums(n + 1, b1_, h1, TPB - 1)
                                elif j in (2, 4, 6):
                                    b2_, h2 = (b, h + 2) if h + 2 < H else (b + 1, h + 2 - H)
                                    row_sums(n + 2, b2_, h2, j // 2 - 1)
                            if h == H - 1:
                                copy_half(n, h)

                @block.tensor
                def _(pe):
                    def piece(n, b, h, u):
                        a, k = u // UPT, u % UPT
                        if u == 0:
                            pe.wait_ge(q_in[h % 4], 16 * (b * (H // 4) + h // 4 + 1))
                            pe.wait_ge(k_in[h], 16)
                        at_least(pe, maxima_read, UNITS * n + u - 1)
                        pe.matmul(ps[:, u % 2, :], qs[0:KR, h % 4, a * P:(a + 1) * P],
                                  ks[0:KR, h, k * 512:(k + 1) * 512], start=True, stop=True)\
                            .then_inc(maxima_scores, 1)

                    def turn_negmax(n, h):
                        pe.wait_ge(negmax_ready, TPB * (n + 1))
                        pe.wait_ge(context_summed, n)
                        pe.transpose(ps[0:TPB, 6 + h % 2, 0:P], negmax[:, h % 2, :], ident[:, :])\
                            .then_inc(negmax_turned, 1)

                    def key_scores(n, b, h, j):
                        if j == 0:
                            pe.wait_ge(shift_rows[h % 4], 32 * (b * (H // 4) + h // 4 + 1))
                        if h == 0:
                            pe.wait_ge(maskB_ready, H * b + j + 1)
                        at_least(pe, weights_ready, 8 * n + j)
                        for i in range(2):
                            bank = ps[:, 2 + 2 * (j % 2) + i, :]
                            pe.matmul(bank, ks[:, h, (2 * j + i) * P:(2 * j + i + 1) * P], qs[:, h % 4, :],
                                      start=True, stop=False)
                            mm = pe.matmul(bank, identb[:, :], maskB[:, b % 2, 2 * j + i, :], start=False, stop=True)
                        mm.then_inc(scores_ready, 1)

                    def add_context(n, h, j):
                        pe.wait_ge(weights_ready, 8 * n + j + 2)
                        for i in range(2):
                            for t in range(2):
                                at = (2 * i + t) * HD
                                mm = pe.matmul(ps[at:at + HD, 6 + h % 2, 0:TB // 2],
                                               v_all[:, 2 * j + i, h * HD:(h + 1) * HD],
                                               weights[:, j % 2, i, t * (TB // 2):(t + 1) * (TB // 2)],
                                               start=(j == 0), stop=(j == 7), tile_position=(0, at))
                        mm.then_inc(context_added, 1)

                    for u in range(UNITS):
                        piece(0, 0, 0, u)
                    pe.wait_ge(negmax_ready, TPB)
                    pe.transpose(ps[0:TPB, 6, 0:P], negmax[:, 0, :], ident[:, :]).then_inc(negmax_turned, 1)
                    for u in range(UNITS):
                        piece(1, 0, 1, u)
                    pe.wait_ge(ones_ready, 1)
                    key_scores(0, 0, 0, 0)
                    with pe.Fori(0, NB) as b:
                        for h in range(H):
                            n = b * H + h
                            b1_, h1 = (b, h + 1) if h + 1 < H else (b + 1, 0)
                            b2_, h2 = (b, h + 2) if h + 2 < H else (b + 1, h + 2 - H)
                            for j in range(8):
                                piece(n + 2, b2_, h2, 2 * j)
                                if j < 7:
                                    key_scores(n, b, h, j + 1)
                                else:
                                    key_scores(n + 1, b1_, h1, 0)
                                piece(n + 2, b2_, h2, 2 * j + 1)
                                add_context(n, h, j)
                                if j == 3:
                                    turn_negmax(n + 1, h1)
        ph12.close()

        TOPK = 2
        NBLK = TOPK * T // P + E
        REGION = T + P
        ROW = 272
        expert_rows = dram("expert_rows", [E * REGION + P, ROW], F32)
        sum_rows = dram("sum_rows", [T + P, D], F32)
        assert (F, HE) == (1024, 1024)
        SETS = E + 1
        SPLIT3 = 6
        WC = DC * HE

        ph34 = ExitStack()
        ctx.enter_context(ph34)

        def s34(name, shape, dt):
            return sb(name, shape, dt, ph34)
        wall = s34("wall", [P, SETS, 2, 2, WC], F16)
        wst = s34("wst", [P, 2, WC], F32)
        pad = s34("pad", [P, ROW], F32)
        b1s = s34("b1s", [P, E, HC], F32)
        b2b = s34("b2b", [P, E, D], F32)
        table = s34("table", [P, 2, NBLK + 2], I32)
        c_in = sem("c_in")
        wst_in = [sem("wst_in0"), sem("wst_in1")]
        wst_high = [sem("wst_high0"), sem("wst_high1")]
        wst_split = [sem("wst_split0"), sem("wst_split1")]

        def up(s, part, c, m):
            return wall[:, s, 0, part, c * HE + m * P:c * HE + (m + 1) * P]

        def down(s, part, m):
            return wall[:, s, 1, part, m * D:(m + 1) * D]

        def load_stage(sp, s, n):
            sp.wait_ge(wst_split[n], s)
            sp.dma_start(wst[:, n, :].rearrange("p (c n) -> p c n", n=(HE, D)[n]),
                         (w1T, w2T)[n][s - 1, :, :].rearrange("(c p) n -> p c n", p=P)).then_inc(wst_in[n], 16)

        def stage_high(act, s, n):
            act.wait_ge(wst_in[n], 16 * s + 16)
            act.activation(wall[:, s, n, 0, :], wst[:, n, :], ACT.Copy, scale=WSCALE).then_inc(wst_high[n], 1)

        def stage_low(dve, s, n):
            dve.wait_ge(wst_high[n], s + 1)
            dve.scalar_tensor_tensor(out=wall[:, s, n, 1, :], in0=wst[:, n, :], scalar=WSCALE,
                                     in1=wall[:, s, n, 0, :], op0=ALU.mult, op1=ALU.subtract)\
                .then_inc(wst_split[n], 1)

        def beside(p, i, bb):
            return 1 + 3 * bb + (3 * p + i) // 2, (3 * p + i) % 2

        ph3 = ExitStack()
        with ph3:
            def s3(name, shape, dt):
                return sb(name, shape, dt, ph3)
            spare = wall[:, SETS - 2:SETS, :, :, :].rearrange("p s n h c -> p (s n h c)").bitcast(F32)
            at = [0]

            def from_spare(*shape):
                size = 1
                for d in shape:
                    size *= d
                v = spare[:, at[0]:at[0] + size]
                at[0] += size
                return v.rearrange("p (a b) -> p a b", a=shape[0]) if len(shape) == 2 else \
                    v.rearrange("p (a b c) -> p a b c", a=shape[0], b=shape[1])
            cT = from_spare(DC, TB)
            rT = from_spare(DC, TB)
            htb = from_spare(2, TPB, D)
            xb = from_spare(2, TPB, D)
            g32 = from_spare(2, TB)
            xnT = from_spare(DC, TB)
            assert at[0] <= spare.shape[1]
            inv = s3("inv", [P, NB * H, TPB], F32)
            inv_turned = s3("inv_turned", [P, P], F32)
            wo = s3("wo", [P, DC, D], F32)
            gw = s3("gw", [P, DC, E], F32)
            bo_b = s3("bo_b", [P, D], F32)
            s2_b = s3("s2_b", [P, D], F32)
            sh2_b = s3("sh2_b", [P, D], F32)
            hT = s3("hT", [P, 2, 2, DC, TB], F16)
            gT = s3("gT", [P, 2, 2, TB], F16)
            rows = s3("rows", [P, TPB, ROW], F32)
            st3 = s3("st3", [P, 2, TPB, 6], F32)
            mo3 = s3("mo3", [P, 2, 8, TPB], F32)
            logits = s3("logits", [P, TPB, E], F32)
            top = s3("top", [P, 2, TPB], F32)
            key = s3("key", [P, TPB, E], F32)
            keymax = s3("keymax", [P, TPB], F32)
            gap = s3("gap", [P, 5, TPB], F32)
            hot = s3("hot", [P, 2, TPB, E], F32)
            wgt = s3("wgt", [P, 2, TPB, E], F32)
            member = s3("member", [P, TPB, E], BF16)
            rank = s3("rank", [P, TPB, E], F32)
            picked = s3("picked", [P, 2, TPB, E], F32)
            slotf = s3("slotf", [P, 2, TPB], F32)
            slots = s3("slots", [P, 2, TPB], U32)
            place = s3("place", [P, E], F32)
            down_from_e = s3("down_from_e", [P, E], F32)
            u3 = s3("u3", [P, TPB, D], F32)
            y3 = s3("y3", [P, TPB, D], F32)
            credit3 = s3("credit3", [P, 8], F32)
            region0 = s3("region0", [P, E], F32)
            tokens = s3("tokens", [P, NT], F32)
            blocks = s3("blocks", [P, NBLK + 2], F32)
            before = s3("before", [P, P], BF16)
            onesb = s3("onesb", [P, P], BF16)
            minus_half4 = minus_half[:, 0:TPB]
            nblk = s3("nblk", [P, 4, E], F32)
            counts = s3("counts", [P, 3, E], I32)
            ends = s3("ends", [P, E], F32)
            past = s3("past", [P, 2, NBLK + 2, E], F32)
            tabf = s3("tabf", [P, 5, NBLK + 2], F32)

            wsmall_in = sem("wsmall_in")
            ctx_in = sem("ctx_in")
            sums_in = sem("sums_in")
            inv_ready = sem("inv_ready")
            inv_turn = sem("inv_turn")
            inv_copied = sem("inv_copied")
            inv_out = sem("inv_out")
            inv_in = sem("inv_in")
            ctx_scaled = sem("ctx_scaled")
            h3_in = [sem("h3_in0"), sem("h3_in1")]
            x3_in = [sem("x3_in0"), sem("x3_in1")]
            c3_step = sem("c3_step")
            c3_ready = sem("c3_ready")
            attn_ready = sem("attn_ready")
            link_a = sem("link_a")
            link_t = sem("link_t")
            link_e = sem("link_e")
            var3 = [sem("var3A"), sem("var3T")]
            rstd3 = [sem("rstd3A"), sem("rstd3T")]
            h2_ready = sem("h2_ready")
            h2_scaled = sem("h2_scaled")
            h2T_ready = sem("h2T_ready")
            h2T_high = sem("h2T_high")
            h2T_split = sem("h2T_split")
            up_ready = sem("up_ready")
            gelu_ready = sem("gelu_ready")
            g_high = sem("g_high")
            g_split = sem("g_split")
            down_done = sem("down_done")
            x1_ready = sem("x1_ready")
            x1_out = [sem("x1_out0"), sem("x1_out1")]
            xn_ready = sem("xn_ready")
            xnT_ready = sem("xnT_ready")
            xnT_copied = sem("xnT_copied")
            gates_ready = sem("gates_ready")
            gates_read = sem("gates_read")
            rank_read = sem("rank_read")
            gap_ready = sem("gap_ready")
            gap_exp = sem("gap_exp")
            member_ready = sem("member_ready")
            rows_ready = sem("rows_ready")
            rank_ready = sem("rank_ready")
            slots_ready = sem("slots_ready")
            scattered = sem("scattered")
            table_ready = sem("table_ready")
            pads_out = sem("pads_out")

            block = nc.Block()
            with block:
                @block.sync
                def _(sp):
                    inv_flat = inv_sums.rearrange("r p -> (r p)")

                    def load_inv(b):
                        for h in range(H):
                            at = h % (H // DC) * HD
                            sp.dma_start(rT[at:at + HD, h // (H // DC), :],
                                         inv_flat[bass.ds((b * H + h) * TB, TB)].partition_broadcast(HD)).then_inc(inv_in, 16)

                    sp.dma_start(inv[:, :, :], sums[:, 0:NB * H, :]).then_inc(sums_in, 16)
                    sp.dma_start(cT[:, :, :], ctx_cols[:, 0:TB].rearrange("(c p) t -> p c t", p=P)).then_inc(ctx_in, 16)
                    sp.dma_start(wo[:, :, :], Wo.rearrange("(c p) n -> p c n", p=P)).then_inc(wsmall_in, 16)
                    sp.dma_start(bo_b[:, :], bo.partition_broadcast(P)).then_inc(wsmall_in, 16)

                    def load_h(b, p):
                        sp.dma_start(htb[:, p, :, :], ht_rows[bass.ds(b * TB, TB), :]
                                     .rearrange("(a p) d -> p a d", p=P)).then_inc(h3_in[p], 16)

                    def load_x(b, p):
                        sp.dma_start(xb[:, p, :, :], x[bass.ds(b * TB, TB), :]
                                     .rearrange("(a p) d -> p a d", p=P)).then_inc(x3_in[p], 16)
                    load_h(0, 0)
                    sp.dma_start(s2_b[:, :], ln2_scale.partition_broadcast(P)).then_inc(wsmall_in, 16)
                    sp.dma_start(sh2_b[:, :], ln2_bias.partition_broadcast(P)).then_inc(wsmall_in, 16)
                    sp.dma_start(gw[:, :, :], gate_wT.rearrange("(c p) e -> p c e", p=P)).then_inc(wsmall_in, 16)
                    sp.wait_ge(inv_copied, 1)
                    sp.dma_start(inv_sums[:, :], inv_turned[:, :]).then_inc(inv_out, 16)
                    sp.wait_ge(inv_out, 16)
                    load_inv(0)
                    for n, w in enumerate((W1, W2)):
                        sp.dma_start(wst[:, n, :].rearrange("p (c n) -> p c n", n=(F, D)[n]),
                                     w.rearrange("(c p) n -> p c n", p=P)).then_inc(wst_in[n], 16)
                    load_x(0, 0)
                    load_h(1, 1)
                    load_x(1, 1)
                    sp.dma_start(b1s[:, :, :], b1).then_inc(c_in, 16)
                    sp.dma_start(b2b[:, :, :], b2.rearrange("e d -> (e d)").partition_broadcast(P)).then_inc(c_in, 16)
                    def load_context(b, at):
                        wait_apart(sp, attn_ready, TPB * b)
                        sp.dma_start(cT[:, :, :], ctx_cols[:, bass.ds(at * TB, TB)]
                                     .rearrange("(c p) t -> p c t", p=P)).then_inc(ctx_in, 16)
                        load_inv(at)

                    def store_x1(b, bb, p):
                        sp.wait_ge(x1_ready, TPB * (b + 1) + 1)
                        load_h((b + 2) % NB, p)
                        sp.dma_start(sum_rows[bass.ds(b * TB, TB), :].rearrange("(a p) d -> p a d", p=P),
                                     xb[:, p, :, :]).then_inc(x1_out[p], 16)
                        sp.wait_ge(x1_out[p], 16 * (bb + 1))
                        sp.wait_ge(xn_ready, TPB * (b + 1))
                        load_x((b + 2) % NB, p)

                    load_context(1, 1)
                    with sp.Fori(0, NB // 2) as bb:
                        for p in range(2):
                            b = 2 * bb + p
                            for i in range(3):
                                if i == 2:
                                    load_context(b + 2, (b + 2) % NB)
                                    if p:
                                        store_x1(b - 1, bb, 0)
                                load_stage(sp, *beside(p, i, bb))
                            if p:
                                store_x1(b, bb, 1)
                    sp.wait_ge(table_ready, 1)
                    for e in range(E):
                        r = sp.value_load(counts[0:1, 0, e:e + 1], min_val=0, max_val=T)
                        sp.dma_start(expert_rows[bass.ds(r + e * REGION, P), :], pad[:, :]).then_inc(pads_out, 16)
                    sp.wait_ge(pads_out, 16 * E)
                    sp.wait_ge(ctx_in, 16 * (NB + 2))
                    sp.wait_ge(inv_in, 16 * H * (NB + 2))
                    sp.wait_ge(c_in, 32)
                    for p in range(2):
                        sp.wait_ge(h3_in[p], 16 * (NB // 2 + 1))
                        sp.wait_ge(x3_in[p], 16 * (NB // 2 + 1))

                @block.gpsimd
                def _(pool):
                    pool.memset(pad[:, :], 0.0).then_inc(c3_step, 1)
                    pool.wait_ge(c3_step, 1)
                    pool.iota(pad[:, D + E:D + E + 1], pattern=[[0, 1]], base=T, channel_multiplier=1,
                              allow_small_or_imprecise_dtypes=True).then_inc(c3_ready, 1)
                    pool.iota(tokens[:, :], pattern=[[P, NT]], base=0, channel_multiplier=1,
                              allow_small_or_imprecise_dtypes=True).then_inc(c3_ready, 1)
                    pool.iota(down_from_e[:, :], pattern=[[-1, E]], base=E, channel_multiplier=0,
                              allow_small_or_imprecise_dtypes=True).then_inc(c3_ready, 1)
                    pool.iota(region0[:, :], pattern=[[REGION, E]], base=0, channel_multiplier=0,
                              allow_small_or_imprecise_dtypes=True).then_inc(c3_ready, 1)
                    pool.iota(blocks[:, :], pattern=[[1, NBLK + 2]], base=0, channel_multiplier=0,
                              allow_small_or_imprecise_dtypes=True).then_inc(c3_ready, 1)
                    pool.memset(onesb[:, :], 1.0).then_inc(c3_ready, 1)
                    pool.memset(rows[:, :, D + E:ROW], 0.0).then_inc(c3_ready, 1)
                    pool.wait_ge(c3_ready, 7)
                    pool.affine_select(out=before[:, :], in_=onesb[:, :], compare_op=ALU.is_gt, fill=0.0, base=0,
                                       pattern=[[1, P]], channel_multiplier=-1).then_inc(c3_ready, 1)

                    pool.wait_ge(c3_ready, 8)
                    pool.dma_start(expert_rows[E * REGION:E * REGION + P, :], pad[:, :]).then_inc(scattered, 16)

                    def inverse_root(k, b):
                        pool.wait_ge(var3[k], b + 1)
                        pool.tensor_tensor(mo3[:, k, 7, :], mo3[:, k, 6, :], minus_half[:, 0:TPB], ALU.pow)\
                            .then_inc(rstd3[k], 1)

                    def scatter(b):
                        wait_apart(pool, rows_ready, 2 * b + 2)
                        pool.wait_ge(slots_ready, 2 * b + 2)
                        for a in range(TPB):
                            for k in range(TOPK):
                                pool.indirect_dma_start(
                                    out=expert_rows[:, :], in_=rows[:, a, :], in_offset=None,
                                    out_offset=bass.IndirectOffsetOnAxis(ap=slots[:, k, a:a + 1], axis=0),
                                    bounds_check=E * REGION + P - 1).then_inc(scattered, 16)

                    def scale_context(b):
                        pool.wait_ge(ctx_in, 16 * b + 16)
                        pool.wait_ge(inv_in, 16 * H * (b + 1))
                        pool.tensor_tensor(cT[:, :, :], cT[:, :, :], rT[:, :, :], ALU.mult).then_inc(ctx_scaled, 1)

                    scale_context(0)
                    inverse_root(0, 0)
                    scale_context(1)
                    with pool.Fori(0, NB // 2) as bb:
                        b = 2 * bb
                        inverse_root(0, b + 1)
                        scale_context(b + 2)
                        inverse_root(1, b)
                        inverse_root(0, b + 2)
                        scale_context(b + 3)
                        scatter(b)
                        inverse_root(1, b + 1)
                        scatter(b + 1)
                    pool.wait_ge(scattered, 16 * (TOPK * NT + 1))

                @block.vector
                def _(dve):
                    def chain(signal, length):
                        at_block, marked = [0], [0]

                        def begin(b):
                            at_block[0], marked[0] = b, 0

                        def mark(ins):
                            marked[0] += 1
                            ins.then_inc(signal, 1)

                        def settle():
                            dve.wait_ge(signal, length * at_block[0] + marked[0])

                        def end():
                            assert marked[0] == length, (marked[0], length)
                        return begin, mark, settle, end

                    A_LEN = 4 * TPB + 7
                    T_LEN = 2 * TPB + 26
                    begin_A, mark_A, settle_A, end_A = chain(link_a, A_LEN)
                    begin_T, mark_T, settle_T, end_T = chain(link_t, T_LEN)

                    def moments(k, mark, settle):
                        m = mo3[:, k, :, :]
                        e, o = st3[:, k, :, 1], st3[:, k, :, 4]
                        mark(dve.tensor_tensor(m[:, 0, :], e, o, ALU.add))
                        mark(dve.tensor_tensor(m[:, 1, :], e, o, ALU.subtract))
                        mark(dve.tensor_tensor(m[:, 2, :], st3[:, k, :, 2], st3[:, k, :, 5], ALU.add))
                        settle()
                        mark(dve.tensor_scalar(m[:, 3, :], m[:, 0, :], 0.5, None, ALU.mult))
                        mark(dve.tensor_tensor(m[:, 4, :], m[:, 1, :], m[:, 1, :], ALU.mult))
                        settle()
                        mark(dve.tensor_scalar(m[:, 5, :], m[:, 4, :], 0.25, EPS, ALU.mult, ALU.add))
                        settle()
                        dve.scalar_tensor_tensor(out=m[:, 6, :], in0=m[:, 2, :], scalar=1.0 / D, in1=m[:, 5, :],
                                                 op0=ALU.mult, op1=ALU.add).then_inc(var3[k], 1)

                    def attention_sum(b, p, at, loads):
                        begin_A(b)
                        dve.wait_ge(h3_in[p], loads)
                        for a in range(TPB):
                            dve.wait_ge(attn_ready, TPB * b + 2 * (a // 2) + 2)
                            mark_A(dve.tensor_tensor(u3[:, a, :], ps[:, 2 + a // 2, a % 2 * D:(a % 2 + 1) * D],
                                                          bo_b[:, :], ALU.add))
                        settle_A()
                        for a in range(TPB):
                            mark_A(dve.scalar_tensor_tensor(out=htb[:, p, a, :], in0=u3[:, a, :],
                                                                 scalar=m01[:, bass.ds(at + a, 1)],
                                                                 in1=htb[:, p, a, :], op0=ALU.mult, op1=ALU.add))
                        settle_A()

                    def attention_moments(p):
                        for a in range(TPB):
                            mark_A(dve.bn_stats(st3[:, 0, a, :], htb[:, p, a, :]))
                        settle_A()
                        moments(0, mark_A, settle_A)

                    def second_norm(b, p, at):
                        dve.wait_ge(rstd3[0], b + 1)
                        mark_A(dve.tensor_tensor(mo3[:, 0, 5, :], mo3[:, 0, 7, :], m01[:, bass.ds(at, TPB)],
                                                      ALU.mult))
                        settle_A()
                        for a in range(TPB):
                            mark_A(dve.tensor_scalar(u3[:, a, :], htb[:, p, a, :], mo3[:, 0, 3, a:a + 1],
                                                          mo3[:, 0, 5, a:a + 1], ALU.subtract, ALU.mult))
                        settle_A()
                        for a in range(TPB):
                            dve.tensor_tensor(u3[:, a, :], u3[:, a, :], s2_b[:, :], ALU.mult).then_inc(h2_scaled, 1)

                    def second_shift(b, p, at):
                        dve.wait_ge(h2_scaled, TPB * b + TPB)
                        for a in range(TPB):
                            dve.scalar_tensor_tensor(out=htb[:, p, a, :], in0=sh2_b[:, :],
                                                     scalar=m01[:, bass.ds(at + a, 1)], in1=u3[:, a, :],
                                                     op0=ALU.mult, op1=ALU.add).then_inc(h2_ready, 1)
                        end_A()

                    def split_turned(b, p):
                        for c in range(DC):
                            dve.wait_ge(h2T_high, DC * b + c + 1)
                            dve.tensor_tensor(hT[:, p, 1, c, :], ps[:, 2 + c, :], hT[:, p, 0, c, :], ALU.subtract)\
                                .then_inc(h2T_split, 1)

                    def split_hidden(b, f):
                        dve.wait_ge(g_high, FC * b + f + 1)
                        dve.tensor_tensor(gT[:, 1, f % 2, :], g32[:, f % 2, :], gT[:, 0, f % 2, :], ALU.subtract)\
                            .then_inc(g_split, 1)

                    def new_x(b, bb, p):
                        begin_T(b)
                        dve.wait_ge(down_done, FC * b + FC + 2)
                        for a in range(TPB):
                            mark_T(dve.scalar_tensor_tensor(out=y3[:, a, :], in0=ps[:, 4 + a, 0:D],
                                                                 scalar=1.0 / WSCALE, in1=htb[:, p, a, :],
                                                                 op0=ALU.mult, op1=ALU.add))
                        settle_T()
                        dve.wait_ge(x3_in[p], 16 * (bb + 1))
                        for a in range(TPB):
                            dve.tensor_tensor(xb[:, p, a, :], xb[:, p, a, :], y3[:, a, :], ALU.add)\
                                .then_inc(x1_ready, 1)
                        dve.wait_ge(x1_ready, TPB * b + TPB + 1)

                    def new_moments(p):
                        for a in range(TPB):
                            mark_T(dve.bn_stats(st3[:, 1, a, :], xb[:, p, a, :]))
                        settle_T()
                        moments(1, mark_T, settle_T)

                    def expert_rows_of(b, p):
                        dve.wait_ge(rstd3[1], b + 1)
                        dve.wait_ge(scattered, 16 * TOPK * TPB * b + 16)
                        for a in range(TPB):
                            dve.tensor_scalar(rows[:, a, 0:D], xb[:, p, a, :], mo3[:, 1, 3, a:a + 1],
                                              mo3[:, 1, 7, a:a + 1], ALU.subtract, ALU.mult).then_inc(xn_ready, 1)

                    def choose(b):
                        mark = mark_T
                        dve.wait_ge(gates_ready, b + 1)
                        dve.tensor_copy(logits[:, :, :], ps[:, 2, 0:TPB * E].rearrange("p (a e) -> p a e", e=E))\
                            .then_inc(gates_read, 1)
                        dve.wait_ge(gates_read, b + 2)
                        for k in range(TOPK):
                            mark(dve.tensor_reduce(top[:, k, :], logits[:, :, :], AX.X, ALU.max))
                            settle_T()
                            mark(dve.tensor_tensor(key[:, :, :], logits[:, :, :],
                                                   top[:, k, :].unsqueeze(2).to_broadcast([P, TPB, E]), ALU.is_equal))
                            settle_T()
                            mark(dve.tensor_tensor(key[:, :, :], key[:, :, :],
                                                   down_from_e[:, :].unsqueeze(1).to_broadcast([P, TPB, E]),
                                                   ALU.mult))
                            settle_T()
                            mark(dve.tensor_reduce(keymax[:, :], key[:, :, :], AX.X, ALU.max))
                            settle_T()
                            mark(dve.tensor_tensor(hot[:, k, :, :], key[:, :, :],
                                                   keymax[:, :].unsqueeze(2).to_broadcast([P, TPB, E]), ALU.is_equal))
                            settle_T()
                            if k == 0:
                                mark(dve.scalar_tensor_tensor(out=logits[:, :, :], in0=hot[:, 0, :, :], scalar=-3e38,
                                                              in1=logits[:, :, :], op0=ALU.mult, op1=ALU.add))
                                settle_T()
                        dve.tensor_tensor(member[:, :, :], hot[:, 0, :, :], hot[:, 1, :, :], ALU.add)\
                            .then_inc(member_ready, 1)
                        dve.tensor_tensor(gap[:, 0, :], top[:, 1, :], top[:, 0, :], ALU.subtract)\
                            .then_inc(gap_ready, 1)

                    def send(b):
                        mark = mark_T
                        dve.wait_ge(gap_exp, b + 1)
                        mark(dve.tensor_scalar(gap[:, 2, :], gap[:, 1, :], 1.0, None, ALU.add))
                        settle_T()
                        mark(dve.reciprocal(gap[:, 3, :], gap[:, 2, :]))
                        settle_T()
                        mark(dve.tensor_tensor(gap[:, 4, :], gap[:, 3, :], gap[:, 1, :], ALU.mult))
                        settle_T()
                        for k in range(TOPK):
                            mark(dve.tensor_tensor(wgt[:, k, :, :], hot[:, k, :, :],
                                                   gap[:, 3 + k, :].unsqueeze(2).to_broadcast([P, TPB, E]), ALU.mult))
                        settle_T()
                        dve.tensor_tensor(rows[:, :, D:D + E], wgt[:, 0, :, :], wgt[:, 1, :, :], ALU.add)\
                            .then_inc(rows_ready, 1)
                        dve.tensor_copy(rows[:, :, D + E], tokens[:, bass.ds(b * TPB, TPB)]).then_inc(rows_ready, 1)
                        dve.wait_ge(rank_ready, b + 1)
                        mark(dve.tensor_tensor(rank[:, :, :], ps[:, 3, 0:TPB * E].rearrange("p (a e) -> p a e", e=E),
                                               place[:, :].unsqueeze(1).to_broadcast([P, TPB, E]), ALU.add))
                        settle_T()
                        dve.tensor_tensor(place[:, :], place[:, :], ps[:, 3, TPB * E:(TPB + 1) * E], ALU.add)\
                            .then_inc(rank_read, 1)
                        for k in range(TOPK):
                            mark(dve.tensor_tensor(picked[:, k, :, :], hot[:, k, :, :], rank[:, :, :], ALU.mult))
                        settle_T()
                        mark(dve.tensor_reduce(slotf[:, :, :], picked[:, :, :, :], AX.X, ALU.add))
                        settle_T()
                        for k in range(TOPK):
                            dve.tensor_copy(slots[:, k, :], slotf[:, k, :]).then_inc(slots_ready, 1)
                        dve.wait_ge(rank_read, b + 2)
                        end_T()

                    dve.wait_ge(sums_in, 16)
                    dve.reciprocal(inv[:, :, :], inv[:, :, :]).then_inc(inv_ready, 1)
                    dve.wait_ge(inv_turn, 1)
                    dve.tensor_copy(inv_turned[:, :], ps[:, 0, 0:P]).then_inc(inv_copied, 1)
                    dve.wait_ge(c3_ready, 8)
                    dve.tensor_copy(place[:, :], region0[:, :]).then_inc(rank_read, 1)
                    dve.memset(credit3[:, 0:1], 0.0).then_inc(gates_read, 1)
                    dve.memset(credit3[:, 1:2], 0.0).then_inc(x1_ready, 1)
                    for i in range(2):
                        dve.memset(credit3[:, 3 + i:4 + i], 0.0).then_inc(g_split, 1)
                        dve.memset(credit3[:, 5 + i:6 + i], 0.0).then_inc(down_done, 1)
                    dve.wait_ge(rank_read, 1)
                    dve.wait_ge(wsmall_in, 16 * 5)
                    attention_sum(0, 0, 0, 16)
                    attention_moments(0)
                    for n in range(2):
                        stage_low(dve, 0, n)
                    second_norm(0, 0, 0)
                    second_shift(0, 0, 0)
                    split_turned(0, 0)
                    with dve.Fori(0, NB // 2) as bb:
                        b = 2 * bb
                        at = (b + 1) * TPB
                        for f in range(FC):
                            split_hidden(b, f)
                            if f == 0:
                                attention_sum(b + 1, 1, at, 16 * (bb + 1))
                            elif f == 1:
                                attention_moments(1)
                            elif f == 3:
                                second_norm(b + 1, 1, at)
                            elif f == 4:
                                second_shift(b + 1, 1, at)
                            if f in (2, 5, 6):
                                stage_low(dve, *beside(0, (2, 5, 6).index(f), bb))
                        split_turned(b + 1, 1)
                        new_x(b, bb, 0)
                        at = (b + 2) % NB * TPB
                        for f in range(FC):
                            split_hidden(b + 1, f)
                            if f == 0:
                                new_moments(0)
                            elif f == 1:
                                expert_rows_of(b, 0)
                            elif f == 2:
                                attention_sum(b + 2, 0, at, 16 * (bb + 2))
                            elif f == 3:
                                attention_moments(0)
                            elif f == 4:
                                second_norm(b + 2, 0, at)
                            elif f == 5:
                                second_shift(b + 2, 0, at)
                                choose(b)
                            elif f == 7:
                                send(b)
                            if f in (3, 6):
                                stage_low(dve, *beside(1, f // 3 - 1, bb))
                        split_turned(b + 2, 0)
                        new_x(b + 1, bb, 1)
                        new_moments(1)
                        expert_rows_of(b + 1, 1)
                        stage_low(dve, *beside(1, 2, bb))
                        choose(b + 1)
                        send(b + 1)

                    steps = [0]

                    def then(ins):
                        steps[0] += 1
                        ins.then_inc(link_e, 1)
                        dve.wait_ge(link_e, steps[0])
                    cnt, up127 = nblk[:, 0, :], nblk[:, 1, :]
                    then(dve.tensor_tensor(cnt, place[:, :], region0[:, :], ALU.subtract))
                    then(dve.tensor_scalar(up127, cnt, float(P - 1), None, ALU.add))
                    then(dve.tensor_copy(counts[:, 0, :], cnt))
                    then(dve.tensor_copy(counts[:, 1, :], up127))
                    then(dve.tensor_scalar(counts[:, 2, :], counts[:, 1, :], P.bit_length() - 1, None,
                                           ALU.arith_shift_right))
                    then(dve.tensor_copy(nblk[:, 2, :], counts[:, 2, :]))
                    then(dve.tensor_copy(ends[:, 0:1], nblk[:, 2, 0:1]))
                    for e in range(1, E):
                        then(dve.tensor_tensor(ends[:, e:e + 1], ends[:, e - 1:e], nblk[:, 2, e:e + 1], ALU.add))
                    NJ = NBLK + 2
                    then(dve.tensor_tensor(past[:, 0, :, :], blocks[:, :].unsqueeze(2).to_broadcast([P, NJ, E]),
                                           ends[:, :].unsqueeze(1).to_broadcast([P, NJ, E]), ALU.is_ge))
                    then(dve.tensor_tensor(past[:, 1, :, :], past[:, 0, :, :],
                                           nblk[:, 2, :].unsqueeze(1).to_broadcast([P, NJ, E]), ALU.mult))
                    then(dve.tensor_reduce(tabf[:, 0:2, :], past[:, :, :, :], AX.X, ALU.add))
                    then(dve.tensor_tensor(tabf[:, 2, :], blocks[:, :], tabf[:, 1, :], ALU.subtract))
                    then(dve.tensor_scalar(tabf[:, 3, :], tabf[:, 0, :], float(REGION), None, ALU.mult))
                    then(dve.scalar_tensor_tensor(out=tabf[:, 4, :], in0=tabf[:, 2, :], scalar=float(P),
                                                  in1=tabf[:, 3, :], op0=ALU.mult, op1=ALU.add))
                    then(dve.tensor_scalar(table[:, 1, :], tabf[:, 4, :], float(E * REGION), None, ALU.min))
                    dve.tensor_scalar(table[:, 0, :], tabf[:, 0, :], float(E - 1), None, ALU.min)\
                        .then_inc(table_ready, 1)

                @block.scalar
                def _(act):
                    def high_turned(b, p):
                        for c in range(DC):
                            act.wait_ge(h2T_ready, DC * b + c + 1)
                            act.activation(hT[:, p, 0, c, :], ps[:, 2 + c, :], ACT.Copy).then_inc(h2T_high, 1)

                    def hidden_high(b, f):
                        act.wait_ge(g_split, FC * b + f + 1)
                        act.wait_ge(up_ready, FC * b + f + 1)
                        act.activation(g32[:, f % 2, :], ps[:, f % 2, :], ACT.Gelu_apprx_tanh,
                                       scale=1.0 / WSCALE).then_inc(gelu_ready, 1)
                        act.wait_ge(gelu_ready, FC * b + f + 1)
                        act.wait_ge(down_done, FC * b + f + 1)
                        act.activation(gT[:, 0, f % 2, :], g32[:, f % 2, :], ACT.Copy).then_inc(g_high, 1)

                    def copy_xnT(b):
                        act.wait_ge(xnT_ready, b + 1)
                        act.activation(xnT[:, :, :], ps[:, 2:4, :], ACT.Copy).then_inc(xnT_copied, 1)

                    def gap_exponential(b):
                        act.wait_ge(gap_ready, b + 1)
                        act.activation(gap[:, 1, :], gap[:, 0, :], ACT.Exp).then_inc(gap_exp, 1)

                    for n in range(2):
                        stage_high(act, 0, n)
                    high_turned(0, 0)
                    with act.Fori(0, NB // 2) as bb:
                        for p in range(2):
                            b = 2 * bb + p
                            for f in range(FC):
                                hidden_high(b, f)
                                if f in (1, 3, 5):
                                    stage_high(act, *beside(p, f // 2, bb))
                                if p and f == 4:
                                    copy_xnT(b - 1)
                                if p and f == 7:
                                    gap_exponential(b - 1)
                            high_turned(b + 1, 1 - p)
                        copy_xnT(b)
                        gap_exponential(b)

                @block.tensor
                def _(pe):
                    def attention_out(b):
                        pe.wait_ge(ctx_scaled, b + 1)
                        for a in range(TPB):
                            for c in range(DC):
                                mm = pe.matmul(ps[:, 2 + a // 2, a % 2 * D:(a % 2 + 1) * D],
                                               cT[:, c, a * P:(a + 1) * P], wo[:, c, :],
                                               start=(c == 0), stop=(c == DC - 1))
                            mm.then_inc(attn_ready, 1)

                    def turn_h2(b, p):
                        pe.wait_ge(h2_ready, TPB * b + TPB)
                        for c in range(DC):
                            for a in range(TPB):
                                mm = pe.transpose(ps[:, 2 + c, a * P:(a + 1) * P], htb[:, p, a, c * P:(c + 1) * P],
                                                  ident[:, :])
                            mm.then_inc(h2T_ready, 1)

                    def hidden(b, p, f):
                        if f >= 2:
                            pe.wait_ge(gelu_ready, FC * b + f - 1)
                        for n, (w, h) in enumerate(((0, 0), (0, 1), (1, 0))):
                            for c in range(DC):
                                mm = pe.matmul(ps[:, f % 2, :], up(0, w, c, f), hT[:, p, h, c, :],
                                               start=(n == 0 and c == 0), stop=(n == 2 and c == DC - 1))
                        mm.then_inc(up_ready, 1)

                    def back(b, f):
                        pe.wait_ge(g_split, FC * b + f + 3)
                        if f == 0:
                            pe.wait_ge(x1_ready, TPB * b + 1)
                        for a in range(TPB):
                            for n, (g, w) in enumerate(((0, 0), (0, 1), (1, 0))):
                                mm = pe.matmul(ps[:, 4 + a, 0:D], gT[:, g, f % 2, a * P:(a + 1) * P], down(0, w, f),
                                               start=(f == 0 and n == 0), stop=(f == FC - 1 and n == 2))
                        mm.then_inc(down_done, 1)

                    def turn_xn(b):
                        pe.wait_ge(xn_ready, TPB * b + TPB)
                        for c in range(DC):
                            for a in range(TPB):
                                mm = pe.transpose(ps[:, 2 + c, a * P:(a + 1) * P], rows[:, a, c * P:(c + 1) * P],
                                                  ident[:, :])
                        mm.then_inc(xnT_ready, 1)

                    def gates(b):
                        pe.wait_ge(xnT_copied, b + 1)
                        for a in range(TPB):
                            for c in range(DC):
                                mm = pe.matmul(ps[:, 2, a * E:(a + 1) * E], xnT[:, c, a * P:(a + 1) * P],
                                               gw[:, c, :], start=(c == 0), stop=(c == DC - 1))
                        mm.then_inc(gates_ready, 1)

                    def ranks(b):
                        pe.wait_ge(member_ready, b + 1)
                        for a in range(TPB):
                            for k in range(a + 1):
                                pe.matmul(ps[:, 3, a * E:(a + 1) * E], (before if k == a else onesb)[:, :],
                                          member[:, k, :], start=(k == 0), stop=(k == a))
                        for k in range(TPB):
                            mm = pe.matmul(ps[:, 3, TPB * E:(TPB + 1) * E], onesb[:, :], member[:, k, :],
                                           start=(k == 0), stop=(k == TPB - 1))
                        mm.then_inc(rank_ready, 1)

                    pe.wait_ge(inv_ready, 1)
                    pe.transpose(ps[:, 0, 0:P], inv[:, :, :].rearrange("p n t -> p (n t)"), ident[:, :])\
                        .then_inc(inv_turn, 1)
                    pe.wait_ge(wsmall_in, 16 * 5)
                    pe.wait_ge(c3_ready, 8)
                    attention_out(0)
                    turn_h2(0, 0)
                    pe.wait_ge(inv_copied, 1)
                    for n in range(2):
                        pe.wait_ge(wst_split[n], 1)
                    with pe.Fori(0, NB // 2) as bb:
                        b = 2 * bb
                        pe.wait_ge(h2T_split, DC * (b + 1))
                        pe.wait_ge(gates_read, b + 1)
                        pe.wait_ge(rank_read, b + 1)
                        attention_out(b + 1)
                        hidden(b, 0, 0)
                        for f in range(FC):
                            if f + 1 < FC:
                                hidden(b, 0, f + 1)
                            back(b, f)
                            if f == 5:
                                turn_h2(b + 1, 1)
                        pe.wait_ge(h2T_split, DC * (b + 2))
                        attention_out(b + 2)
                        hidden(b + 1, 1, 0)
                        for f in range(FC):
                            if f + 1 < FC:
                                hidden(b + 1, 1, f + 1)
                            back(b + 1, f)
                            if f == 3:
                                pe.wait_ge(var3[0], b + 3)
                                turn_xn(b)
                            elif f == 4:
                                gates(b)
                            elif f == 6:
                                ranks(b)
                            elif f == 7:
                                pe.wait_ge(gates_read, b + 2)
                                pe.wait_ge(rank_read, b + 2)
                                turn_h2(b + 2, 0)
                        pe.wait_ge(h2T_split, DC * (b + 3))
                        turn_xn(b + 1)
                        gates(b + 1)
                        ranks(b + 1)

        ph4 = ExitStack()
        with ph4:
            def s4(name, shape, dt):
                return sb(name, shape, dt, ph4)
            xr = s4("xr", [P, 2, ROW], F32)
            meta = s4("meta", [P, 2, ROW - D], F32)
            xT = s4("xT", [P, 2, 2, D], F16)
            g4 = s4("g4", [P, 2, HE], F32)
            gT4 = s4("gT4", [P, 2, 2, HE], F16)
            y4 = s4("y4", [P, 2, D], F32)
            ids = s4("ids", [P, 2, 1], U32)
            credit4 = s4("credit4", [P, 2], F32)

            row_in = [sem("row_in0"), sem("row_in1")]
            xT_ready = sem("xT_ready")
            xT_high = sem("xT_high")
            xT_split = sem("xT_split")
            mid_ready = sem("mid_ready")
            mid_gelu = sem("mid_gelu")
            mid_high = sem("mid_high")
            mid_split = sem("mid_split")
            end_ready = sem("end_ready")
            y_step = sem("y_step")
            y_ready = sem("y_ready")
            meta_ready = sem("meta_ready")
            added = [sem("added0"), sem("added1")]
            out_done = sem("out_done")
            LATE = range(SPLIT3 + 1, SETS)

            def first_row(eng, j):
                return eng.value_load(table[0:1, 1, bass.ds(j, 1)], min_val=0, max_val=E * REGION)

            def expert(eng, j):
                return eng.value_load(table[0:1, 0, bass.ds(j, 1)], min_val=0, max_val=E - 1)

            block = nc.Block()
            with block:
                @block.sync
                def _(sp):
                    for q in range(2):
                        sp.dma_start(xr[:, q, :], expert_rows[bass.ds(first_row(sp, q), P), :]).then_inc(row_in[q], 16)
                    for s in LATE:
                        for n in range(2):
                            load_stage(sp, s, n)
                    with sp.Fori(0, NBLK // 2) as jj:
                        for q in range(2):
                            j = 2 * jj + q
                            sp.wait_ge(xT_ready, j + 1)
                            sp.wait_ge(meta_ready, j + 1)
                            sp.dma_start(xr[:, q, :], expert_rows[bass.ds(first_row(sp, j + 2), P), :])\
                                .then_inc(row_in[q], 16)
                    for q in range(2):
                        sp.wait_ge(added[q], 16 * (NBLK // 2 + 1))
                    sp.dma_start(out[:, :], sum_rows[0:T, :]).then_inc(out_done, 16)
                    sp.wait_ge(out_done, 16)
                    for q in range(2):
                        sp.wait_ge(row_in[q], 16 * (NBLK // 2 + 1))

                @block.gpsimd
                def _(pool):
                    for i in range(2):
                        pool.dma_start(sum_rows[T + i * (P // 2):T + (i + 1) * (P // 2), :],
                                       pad[i * (P // 2):(i + 1) * (P // 2), 0:D]).then_inc(added[i], 16)
                    with pool.Fori(0, NBLK // 2) as jj:
                        for q in range(2):
                            j = 2 * jj + q
                            pool.wait_ge(y_step, 2 * j + 2)
                            pool.wait_ge(y_ready, j + 3)
                            wait_apart(pool, added[1 - q], 16 * (jj + 1 + q))
                            pool.indirect_dma_start(
                                out=sum_rows[:, :], in_=y4[:, q, :], in_offset=None,
                                out_offset=bass.IndirectOffsetOnAxis(ap=ids[:, q, :], axis=0),
                                bounds_check=T + P - 1, compute_op=ALU.add).then_inc(added[q], 16)

                @block.vector
                def _(dve):
                    def low_rows(j, q):
                        dve.wait_ge(xT_high, j + 1)
                        dve.tensor_tensor(xT[:, q, 1, :], ps[:, 6 + q, 0:D], xT[:, q, 0, :], ALU.subtract)\
                            .then_inc(xT_split, 1)

                    def keep_meta(j, q, loads):
                        dve.wait_ge(row_in[q], loads)
                        dve.tensor_copy(meta[:, q, :], xr[:, q, D:ROW]).then_inc(meta_ready, 1)

                    def low_hidden(j, q):
                        dve.wait_ge(mid_high, j + 1)
                        dve.tensor_tensor(gT4[:, 1, q, :], g4[:, q, :], gT4[:, 0, q, :], ALU.subtract)\
                            .then_inc(mid_split, 1)

                    for i in range(2):
                        dve.memset(credit4[:, i:i + 1], 0.0).then_inc(y_ready, 1)
                    for q in range(2):
                        low_rows(q, q)
                        keep_meta(q, q, 16)
                    for n in range(2):
                        stage_low(dve, LATE[0], n)
                    low_hidden(0, 0)
                    for n in range(2):
                        stage_low(dve, LATE[1], n)
                    dve.wait_ge(c_in, 32)
                    with dve.Fori(0, NBLK // 2) as jj:
                        for q in range(2):
                            j = 2 * jj + q
                            low_rows(j + 2, q)
                            low_hidden(j + 1, 1 - q)
                            e = expert(dve, j)
                            dve.wait_ge(end_ready, j + 1)
                            dve.wait_ge(added[q], 16 * (jj + 1))
                            dve.scalar_tensor_tensor(out=y4[:, q, :], in0=ps[:, 4 + q, 0:D], scalar=1.0 / WSCALE,
                                                     in1=b2b[:, e, :], op0=ALU.mult, op1=ALU.add)\
                                .then_inc(y_step, 1)
                            dve.wait_ge(meta_ready, j + 1)
                            dve.tensor_copy(ids[:, q, :], meta[:, q, E:E + 1]).then_inc(y_step, 1)
                            dve.wait_ge(y_step, 2 * j + 2)
                            dve.tensor_scalar(y4[:, q, :], y4[:, q, :], meta[:, q, bass.ds(e, 1)], None, ALU.mult)\
                                .then_inc(y_ready, 1)
                            dve.wait_ge(y_ready, j + 3)
                            keep_meta(j + 2, q, 16 * (jj + 2))

                @block.scalar
                def _(act):
                    def high_rows(j, q):
                        act.wait_ge(xT_ready, j + 1)
                        act.activation(xT[:, q, 0, :], ps[:, 6 + q, 0:D], ACT.Copy).then_inc(xT_high, 1)

                    def middle(j, q):
                        e = expert(act, j)
                        for m in range(HC):
                            if m % 4 == 0:
                                act.wait_ge(mid_ready, 2 * j + m // 4 + 1)
                            act.activation(g4[:, q, m * P:(m + 1) * P],
                                           ps[:, 2 * q + m // 4, m % 4 * P:(m % 4 + 1) * P], ACT.Gelu,
                                           bias=b1s[:, e, m:m + 1], scale=1.0 / WSCALE).then_inc(mid_gelu, 1)
                        act.wait_ge(mid_gelu, HC * j + HC)
                        act.activation(gT4[:, 0, q, :], g4[:, q, :], ACT.Copy).then_inc(mid_high, 1)

                    for n in range(2):
                        stage_high(act, LATE[0], n)
                    act.wait_ge(c_in, 32)
                    for q in range(2):
                        high_rows(q, q)
                    middle(0, 0)
                    for n in range(2):
                        stage_high(act, LATE[1], n)
                    with act.Fori(0, NBLK // 2) as jj:
                        for q in range(2):
                            j = 2 * jj + q
                            high_rows(j + 2, q)
                            middle(j + 1, 1 - q)

                @block.tensor
                def _(pe):
                    def turn_rows(j, q, loads):
                        pe.wait_ge(row_in[q], loads)
                        for c in range(DC):
                            mm = pe.transpose(ps[:, 6 + q, c * P:(c + 1) * P], xr[:, q, c * P:(c + 1) * P],
                                              ident[:, :])
                        mm.then_inc(xT_ready, 1)

                    def first_half(j, q, e):
                        s = e + 1
                        for n in range(2):
                            pe.wait_ge(wst_split[n], s + 1)
                        pe.wait_ge(xT_split, j + 1)
                        for m in range(HC):
                            for c in range(DC):
                                for n, (w, x_) in enumerate(((0, 0), (0, 1), (1, 0))):
                                    mm = pe.matmul(ps[:, 2 * q + m // 4, m % 4 * P:(m % 4 + 1) * P],
                                                   up(s, w, c, m), xT[:, q, x_, c * P:(c + 1) * P],
                                                   start=(n == 0 and c == 0), stop=(n == 2 and c == DC - 1))
                            if m % 4 == 3:
                                mm.then_inc(mid_ready, 1)

                    def second_half(j, q, e):
                        s = e + 1
                        pe.wait_ge(mid_split, j + 1)
                        pe.wait_ge(y_ready, j + 1)
                        for m in range(HC):
                            for n, (g, w) in enumerate(((0, 0), (0, 1), (1, 0))):
                                mm = pe.matmul(ps[:, 4 + q, 0:D], gT4[:, g, q, m * P:(m + 1) * P], down(s, w, m),
                                               start=(m == 0 and n == 0), stop=(m == HC - 1 and n == 2))
                        mm.then_inc(end_ready, 1)

                    for q in range(2):
                        turn_rows(q, q, 16)
                    first_half(0, 0, expert(pe, 0))
                    assert NBLK % 4 == 0
                    with pe.Fori(0, NBLK // 4) as jq:
                        this = expert(pe, 4 * jq)
                        for i in range(4):
                            j, q = 4 * jq + i, i % 2
                            following = expert(pe, j + 1)
                            turn_rows(j + 2, q, 16 * (2 * jq + i // 2 + 2))
                            first_half(j + 1, 1 - q, following)
                            second_half(j, q, this)
                            this = following


_ORDER = ["x", "adj", "adjT", "nodemask", "L0_gnn_h_target", "L0_gnn_ln1_scale", "L0_gnn_ln1_bias", "L0_gnn_Wq",
          "L0_gnn_bq", "L0_gnn_Wk", "L0_gnn_bk", "L0_gnn_Wv", "L0_gnn_bv", "L0_gnn_Wo", "L0_gnn_bo",
          "L0_gnn_ln2_scale", "L0_gnn_ln2_bias", "L0_gnn_W1", "L0_gnn_W2", "gate_wT", "w1T", "L0_ffn_b1", "w2T",
          "L0_ffn_b2"]


def layout(**inputs):
    import numpy as np

    a = {k: np.ascontiguousarray(v) for k, v in inputs.items()}
    a["adjT"] = np.ascontiguousarray(a["adj"].T)
    a["gate_wT"] = np.ascontiguousarray(a.pop("L0_ffn_gate_w").T)
    a["w1T"] = np.ascontiguousarray(a.pop("L0_ffn_w1").transpose(0, 2, 1))
    a["w2T"] = np.ascontiguousarray(a.pop("L0_ffn_w2").transpose(0, 2, 1))
    b1 = a["L0_ffn_b1"]
    a["L0_ffn_b1"] = np.ascontiguousarray(b1.reshape(b1.shape[0], -1, 128).transpose(2, 0, 1))
    return {f"in_{k}": a[k] for k in _ORDER}


def declare(nc, arrays):
    args = [nc.dram_tensor(k, a.shape, mybir.dt.from_np(a.dtype), kind="ExternalInput").ap()
            for k, a in arrays.items()]
    shape = arrays["in_x"].shape
    return args + [nc.dram_tensor("out_rows", shape, F32, kind="ExternalOutput").ap()]


def kernel(**inputs):
    import concourse.bacc as bacc
    from concourse.bass_utils import run_bass_kernel_spmd

    arrays = layout(**inputs)
    nc = bacc.Bacc("TRN2", target_bir_lowering=False, num_devices=1)
    graph_attention_and_experts(nc, *declare(nc, arrays))
    return run_bass_kernel_spmd(nc, [arrays], core_ids=[0]).results[0]["out_rows"]
```
